# Optimizing a Trainium2 kernel written in Bass

```python
import numpy as np
import jax
import jax.numpy as jnp

def _softmax(x, axis=-1):
    return jax.nn.softmax(x, axis=axis)

def _gelu(x):
    return jax.nn.gelu(x, approximate=True)

def _silu(x):
    return jax.nn.silu(x)

def _sigmoid(x):
    return jax.nn.sigmoid(x)

def _layernorm(x, axis=-1, eps=1e-05):
    m = jnp.mean(x, axis=axis, keepdims=True)
    v = jnp.var(x, axis=axis, keepdims=True)
    return (x - m) / jnp.sqrt(v + eps)

def _scatter_add(tgt, idx, src, axis=0):
    return tgt.at[idx].add(src)

def _segment_sum(src, seg, n):
    return jax.ops.segment_sum(src, seg, n)
kernel_name = 'mk_xattn_ffn_d1_seqx_r4_51124d'

def setup_inputs(seed: int=0):
    np.random.seed(seed)
    _w = jnp.asarray

    def _rec_inputs():
        import jax
        import jax.numpy as jnp
        _rk = jax.random.key(seed)
        x = 7.22e-05 + 1 * jax.random.normal(jax.random.fold_in(_rk, 1), (2, 1024, 256), jnp.float32)
        _lenS = 1024 - jax.random.randint(jax.random.fold_in(_rk, 7), (2,), 0, max(1, 1024 // 4) + 1, jnp.int32)
        _lenS2 = 77 - jax.random.randint(jax.random.fold_in(_rk, 8), (2,), 0, max(1, 77 // 4) + 1, jnp.int32)
        _ctx_1024P = jax.random.normal(jax.random.fold_in(_rk, 11), (2, 16, 256), jnp.float32)
        _ctx_1024c = jax.random.dirichlet(jax.random.fold_in(_rk, 511), 0.3 * jnp.ones((16,), jnp.float32), (2, 77))
        _ctx_1024t = jnp.einsum('bsk,bkd->bsd', _ctx_1024c, _ctx_1024P)
        _ctx_1024t = _ctx_1024t * jax.lax.rsqrt(jnp.mean(jnp.square(_ctx_1024t)) + 1e-12) * 0.953939
        ctx_1024 = 4.13588e-05 + 0.999923 * (_ctx_1024t + 0.3 * jax.random.normal(jax.random.fold_in(_rk, 611), (2, 77, 256), jnp.float32))
        return (x, ctx_1024)
    x, ctx_1024 = _rec_inputs()

    def _L0_xattn_setup():
        import jax, jax.numpy as jnp
        import numpy as np
        N_HEAD = 16
        key = jax.random.key(seed)
        ks = jax.random.split(key, 5)
        b, l, d = (4, 512, 256)
        dh = d // N_HEAD
        return {'q': jax.random.normal(ks[0], (b, l, d), dtype=jnp.float32), 'kv': jax.random.normal(ks[1], (b, l, d), dtype=jnp.float32), 'Wq': jax.random.normal(ks[2], (d, d), dtype=jnp.float32) * 0.02, 'Wkv': jax.random.normal(ks[3], (2 * dh, d), dtype=jnp.float32) * 0.02, 'Wc': jax.random.normal(ks[4], (d, d), dtype=jnp.float32) * 0.02}
    _L0_xattn_all = _L0_xattn_setup()
    _L0_xattn_in = {k: v for k, v in _L0_xattn_all.items() if k in ('Wq', 'Wkv', 'Wc')}
    del _L0_xattn_all

    def _L0_ffn_setup():
        import jax, jax.numpy as jnp
        import numpy as np
        HIDDEN = 256
        INTER = 512
        NUM_EXPERTS = 8
        TOPK = 2
        STD = 0.02
        key = jax.random.key(seed)
        k1, k2, k3, k4 = jax.random.split(key, 4)
        return {'hidden_states': jax.random.normal(k1, (1, 512, HIDDEN), dtype=jnp.float32), 'w1': jax.random.normal(k2, (NUM_EXPERTS, 2 * INTER, HIDDEN), dtype=jnp.float32) * STD, 'w2': jax.random.normal(k3, (NUM_EXPERTS, HIDDEN, INTER), dtype=jnp.float32) * STD, 'router_w': jax.random.normal(k4, (NUM_EXPERTS, HIDDEN), dtype=jnp.float32) * STD}
    _L0_ffn_all = _L0_ffn_setup()
    _L0_ffn_in = {k: v for k, v in _L0_ffn_all.items() if k in ('w1', 'w2', 'router_w')}
    del _L0_ffn_all
    return {'x': x, 'ctx_1024': ctx_1024, 'L0_xattn_Wq': _L0_xattn_in['Wq'], 'L0_xattn_Wkv': _L0_xattn_in['Wkv'], 'L0_xattn_Wc': _L0_xattn_in['Wc'], 'L0_ffn_w1': _L0_ffn_in['w1'], 'L0_ffn_w2': _L0_ffn_in['w2'], 'L0_ffn_router_w': _L0_ffn_in['router_w']}

def reference(x, ctx_1024, L0_xattn_Wq, L0_xattn_Wkv, L0_xattn_Wc, L0_ffn_w1, L0_ffn_w2, L0_ffn_router_w):
    import jax
    import jax.numpy as jnp

    def _L0_xattn_ref(q, kv, Wq, Wkv, Wc):
        import jax, jax.numpy as jnp
        import numpy as np
        N_HEAD = 16
        b, l, d = q.shape
        h = N_HEAD
        dh = d // h
        qp = jnp.einsum('bld,ed->ble', q, Wq)
        scores = jnp.einsum('bld,bmd->blm', qp, kv)
        idx = jnp.argmax(scores, axis=-1)
        mem = jnp.take_along_axis(kv, idx[..., None], axis=1)
        mkv = jnp.einsum('bld,ed->ble', mem, Wkv)
        mk, mv = jnp.split(mkv, 2, axis=-1)
        qh = qp.reshape(b, l, h, dh).transpose(0, 2, 1, 3)
        scale = 1.0 / np.sqrt(dh).astype(np.float32)
        logits = jnp.einsum('bhld,bmd->bhlm', qh, mk) * scale
        attn = jax.nn.softmax(logits, axis=-1)
        out = jnp.einsum('bhlm,bmd->bhld', attn, mv)
        out = out.transpose(0, 2, 1, 3).reshape(b, l, d)
        return jnp.einsum('bld,ed->ble', out, Wc)

    def _L0_ffn_ref(hidden_states, w1, w2, router_w):
        import jax, jax.numpy as jnp
        import numpy as np
        HIDDEN = 256
        INTER = 512
        NUM_EXPERTS = 8
        TOPK = 2
        STD = 0.02
        orig_shape = hidden_states.shape
        dtype = hidden_states.dtype
        x = hidden_states.reshape(-1, orig_shape[-1])
        E = w1.shape[0]
        gating = x @ router_w.T
        probs = jax.nn.softmax(gating.astype(jnp.float32), axis=-1)
        topk_w, sel = jax.lax.top_k(probs, TOPK)
        topk_w = topk_w.astype(dtype)
        combine = (jax.nn.one_hot(sel, E, dtype=dtype) * topk_w[..., None]).sum(axis=1)
        h = jnp.einsum('td,eid->tei', x, w1)
        gate = jax.nn.silu(h[..., :INTER])
        y = h[..., INTER:] * gate
        out = jnp.einsum('tei,ehi,te->th', y, w2, combine)
        return out.reshape(orig_shape)
    x = x + _L0_xattn_ref(_layernorm(x, axis=-1), ctx_1024, L0_xattn_Wq, L0_xattn_Wkv, L0_xattn_Wc)
    x = x + _L0_ffn_ref(_layernorm(x, axis=-1), L0_ffn_w1, L0_ffn_w2, L0_ffn_router_w)
    return x

_drawn_inputs = setup_inputs


def setup_inputs(seed=0):
    import zlib

    import numpy as np

    out = dict(_drawn_inputs(seed))
    spreads = {}
    factors = {'L0_xattn_Wq': 8.0, 'L0_ffn_w1': 8.0, 'L0_ffn_w2': 8.0, 'L0_ffn_router_w': 8.0}
    for name, (base, spread) in spreads.items():
        noise = np.random.default_rng([zlib.crc32(name.encode()), seed]).standard_normal(out[name].shape)
        drawn = base * np.exp(spread * noise) if base else spread * noise
        out[name] = jnp.asarray(drawn.astype(out[name].dtype))
    for name, factor in factors.items():
        out[name] = (out[name] * factor).astype(out[name].dtype)
    return out
```

```python
from contextlib import ExitStack

import concourse.bass as bass
from concourse import mybir

F32 = mybir.dt.float32
F32R = mybir.dt.float32r
F16 = mybir.dt.float16
BF16 = mybir.dt.bfloat16
I32 = mybir.dt.int32
U32 = mybir.dt.uint32
ALU = mybir.AluOpType
ACT = mybir.ActivationFunctionType
AX = mybir.AxisListType
ds = bass.ds

P = 128
D = 256
DC = D // P
B = 2
S = 1024
TB = S // P
T = B * TB
HT = TB // 2
NK = 77
H = 16
DH = D // H
NP = H // 2
HS = P // 2
UH = 32
NG = H // 4
RW = D + 8
WG = D + NK
E = 8
FI = 512
FC = FI // P
BLK = 2 * S * B // P + E - 1
GR = 3
SCALE = 0.25
MASK = -1e30
EPS = 1e-5
assert BLK % GR == 0 and DH ** -0.5 == SCALE

HI_A, LO_A, ONE, HI_B = 0, DH, 2 * DH, 3 * DH


def build(nc, x, ctxT, Wq, WqT, WkvT, WcT, routerT, w1T, w2T, out):
    rows = nc.dram_tensor("rows", [(T + 1) * P, RW], F32).ap()
    with ExitStack() as ctx:
        def sb(name, shape, dt=F32):
            return ctx.enter_context(nc.sbuf_tensor(name, shape, dt))

        def sem(name):
            return ctx.enter_context(nc.semaphore(name))

        ps = ctx.enter_context(nc.psum_tensor("ps", [P, 8, 512], F32))

        iota_f = sb("iota_f", [P, P])
        iota_p = sb("iota_p", [P, 1])
        iota_h = sb("iota_h", [P, P], F16)
        blk_h = sb("blk_h", [P, BLK], F16)
        blk_f = sb("blk_f", [P, BLK])
        tok_h = sb("tok_h", [P, T], F16)
        spare = sb("spare", [P, 1])
        k128 = sb("k128", [P, T])
        desc = sb("desc", [P, NK], BF16)
        desc_e = sb("desc_e", [P, E])
        lt8 = sb("lt8", [P, E, E])
        ident = sb("ident", [P, P])
        tri = sb("tri", [P, P], BF16)
        ones = sb("ones", [P, P], BF16)
        sel_e = sb("sel_e", [P, 1])
        sel_o = sb("sel_o", [P, 1])
        neg = sb("neg", [P, H], F32R)
        half = sb("half", [P, T])
        X = sb("X", [P, T, D])
        WGT = sb("WGT", [P, B, DC, WG])
        WKV = sb("WKV", [P, DC, 2 * DH])
        WC = sb("WC", [P, DC, D])
        RT = sb("RT", [P, DC, E])
        mvb = sb("mvb", [NK, B, DH])
        bd0 = sb("bd0", [P, B, 2 * NK])
        bd = sb("bd", [P, 2 * NK], F32R)
        vc = sb("vc", [NK, UH])
        cc = sb("cc", [NK, 1])
        bias = sb("bias", [P, NK])
        st = sb("st", [P, T, 6])
        mv = sb("mv", [P, T, 2])
        rs = sb("rs", [P, T])
        qs = sb("qs", [P, 2, H, HS])
        qT = sb("qT", [P, NP, S], F32R)
        m1 = sb("m1", [P, TB])
        m2 = sb("m2", [P, TB])
        mT = sb("mT", [P, 2, 512], F32R)
        pT = sb("pT", [P, 8, 512])
        uT = sb("uT", [P, 2, 512])
        rden = sb("rden", [P, HT, 4])
        on = sb("on", [P, HT, D])
        oT = sb("oT", [P, HT, DC, P])
        st2 = sb("st2", [P, HT, 6])
        mv2 = sb("mv2", [P, HT, 2])
        rs2 = sb("rs2", [P, HT])
        xr = sb("xr", [P, HT, RW])
        xn2 = xr[:, :, 0:D]
        rl = sb("rl", [P, HT, E])
        r1 = sb("r1", [P, HT])
        f1 = sb("f1", [P, HT])
        eq = sb("eq", [P, HT, E])
        lm = sb("lm", [P, HT, E])
        ex = sb("ex", [P, HT, E])
        sme = sb("sme", [P, HT])
        o1 = sb("o1", [P, T, E])
        o2 = sb("o2", [P, T, E])
        cnt = sb("cnt", [P, T, E], BF16)
        ce = sb("ce", [P, E, T])
        nb = sb("nb", [P, E])
        cum = sb("cum", [P, E, E])
        end = sb("end", [P, E])
        base = sb("base", [P, E])
        slf = sb("slf", [P, T, E])
        pick = sb("pick", [P, T, E])
        slot = sb("slot", [P, 2, T])
        sloti = sb("sloti", [P, 2 * T], I32)
        bki = sb("bki", [P, 2 * T], I32)
        rmi = sb("rmi", [P, 2 * T], I32)
        bkh = sb("bkh", [P, 2 * T], F16)
        rmf = sb("rmf", [P, 2 * T])
        ebf = sb("ebf", [P, BLK])
        eb = sb("eb", [P, BLK], I32)
        tokp = sb("tokp", [P, BLK])
        idf = sb("idf", [P, BLK])
        idx = sb("idx", [P, BLK], U32)
        W1 = sb("W1", [P, E, DC, 2 * FI])
        W2 = sb("W2", [P, E, FC, D])
        pT1 = pT[:].rearrange("p n q -> p (n q)")
        ns = TB * NK
        sc = pT1[:, 0:ns].rearrange("p (t n) -> p t n", n=NK)
        eqw = pT1[:, ns:3 * ns // 2].bitcast(BF16).rearrange("p (t n) -> p t n", n=NK)
        oh = pT1[:, 3 * ns // 2:2 * ns].bitcast(BF16).rearrange("p (t n) -> p t n", n=NK)
        nh = 2 * T * BLK // 2
        bsel = pT1[:, 0:nh].bitcast(F16).rearrange("p (t b) -> p t b", b=BLK)
        bval = pT1[:, nh:2 * nh].bitcast(F16).rearrange("p (t b) -> p t b", b=BLK)
        ebc = pT1[:, 2 * nh:2 * nh + BLK * E].rearrange("p (b e) -> p b e", e=E)
        asel = pT1[:, 2 * nh + BLK * E:2 * nh + BLK * E + 2 * P].bitcast(F16).rearrange("p (n q) -> p n q", q=P)
        yT = pT1[:, 0:FI].rearrange("p (c q) -> p c q", c=FC)
        xn = on
        xT = oT
        MW = (HT - 1) * H + P
        mx = on[:].rearrange("p t d -> p (t d)")[:, 2 * D:2 * D + 2 * MW].rearrange("p (s n) -> p s n", n=MW)
        ks = oT[0:NK, 2:4].rearrange("p t c q -> p (t c q)").rearrange("p (b o n) -> p b o n", b=B, o=2)
        qs1 = qs[:].rearrange("p s h w -> p (s h w)")
        xg = xr
        xgT = qs1[:, 0:D].rearrange("p (c q) -> p c q", c=DC)
        sg = qs1[:, D:D + FI]
        yb = qs1[:, D + FI:D + 2 * FI]
        ob = oT[:].rearrange("p t c q -> p t (c q)")
        uT1 = uT[:].rearrange("p a b -> p (a b)")
        WQ = uT1[:, 0:DC * D].rearrange("p (c n) -> p c n", c=DC)
        CT = uT1[:, DC * D:DC * (D + B * NK)].rearrange("p (c n) -> p c n", c=DC)

        x_in = [sem(f"x_in{i}") for i in range(B)]
        wts_in = sem("wts_in")
        expw_in = sem("expw_in")
        iotas = sem("iotas")
        consts = sem("consts")
        ln_st = sem("ln_st")
        ln_mv = sem("ln_mv")
        ln_v = sem("ln_v")
        ln_r = sem("ln_r")
        g_mm = sem("g_mm")
        g_out = sem("g_out")
        kv_mm = sem("kv_mm")
        ks_hi = sem("ks_hi")
        ks_ok = sem("ks_ok")
        ks_tr = sem("ks_tr")
        bd0_ok = sem("bd0_ok")
        xn_ok = sem("xn_ok")
        x_tr = sem("x_tr")
        xT_ok = sem("xT_ok")
        q_mm = sem("q_mm")
        q_hi = sem("q_hi")
        q_lo = sem("q_lo")
        sc_ok = sem("sc_ok")
        q_tr = sem("q_tr")
        qTa_ok = sem("qTa_ok")
        qTb_ok = sem("qTb_ok")
        am = sem("am")
        oh_ok = sem("oh_ok")
        cnt_mm = sem("cnt_mm")
        cnt_ok = sem("cnt_ok")
        bd_ok = sem("bd_ok")
        l1_mm = sem("l1_mm")
        mx_ok = sem("mx_ok")
        mx_tr = sem("mx_tr")
        mT_ok = sem("mT_ok")
        l2_mm = sem("l2_mm")
        ex_ok = sem("ex_ok")
        pv_mm = sem("pv_mm")
        ut_ok = sem("ut_ok")
        tu_mm = sem("tu_mm")
        rd_ok = sem("rd_ok")
        on_ok = sem("on_ok")
        o_tr = sem("o_tr")
        oT_ok = sem("oT_ok")
        wc_mm = sem("wc_mm")
        x2_ok = sem("x2_ok")
        st2_ok = sem("st2_ok")
        mv2_ok = sem("mv2_ok")
        v2_ok = sem("v2_ok")
        rs2_ok = sem("rs2_ok")
        xn2_ok = sem("xn2_ok")
        rows_ok = sem("rows_ok")
        rows_out = sem("rows_out")
        x2_out = sem("x2_out")
        x2_tr = sem("x2_tr")
        x2T_ok = sem("x2T_ok")
        r_mm = sem("r_mm")
        top = sem("top")
        cnt_s = sem("cnt_s")
        rl_ok = sem("rl_ok")
        rt = sem("rt")
        lm_ok = sem("lm_ok")
        exr_ok = sem("exr_ok")
        pad_ok = sem("pad_ok")
        pre_mm = sem("pre_mm")
        asel_ok = sem("asel_ok")
        asel_used = sem("asel_used")
        idx_ok = sem("idx_ok")
        eb_ok = sem("eb_ok")
        g_in = [sem(f"g_in{j}") for j in range(GR)]
        gx_tr = sem("gx_tr")
        gxT_ok = sem("gxT_ok")
        h_mm = sem("h_mm")
        sg_ok = sem("sg_ok")
        y_ok = sem("y_ok")
        y_tr = sem("y_tr")
        yT_ok = sem("yT_ok")
        o_mm = sem("o_mm")
        ob_ok = sem("ob_ok")
        sc_out = sem("sc_out")

        block = ctx.enter_context(nc.Block())

        @block.sync
        def _(sp):
            sp.dma_start(X[:, 0:TB, :], x[0:S, :].rearrange("(t p) d -> p t d", p=P)).then_inc(x_in[0], 16)
            sp.dma_start(CT, ctxT.rearrange("(c p) n -> p c n", p=P)).then_inc(wts_in, 16)
            sp.dma_start(WQ[:], Wq.rearrange("(c p) n -> p c n", p=P)).then_inc(wts_in, 16)
            sp.dma_start(WKV[:], WkvT.rearrange("(c p) n -> p c n", p=P)).then_inc(wts_in, 16)
            for b in range(B):
                sp.dma_start(WGT[:, b, :, 0:D], WqT.rearrange("(c p) n -> p c n", p=P)).then_inc(wts_in, 16)
            sp.dma_start(WC[:], WcT.rearrange("(c p) n -> p c n", p=P)).then_inc(wts_in, 16)
            sp.dma_start(RT[:], routerT.rearrange("(c p) n -> p c n", p=P)).then_inc(wts_in, 16)
            sp.dma_start(X[:, TB:T, :], x[S:2 * S, :].rearrange("(t p) d -> p t d", p=P)).then_inc(x_in[1], 16)
            for e in range(E):
                sp.dma_start(W1[:, e], w1T[e].rearrange("(c p) n -> p c n", p=P)).then_inc(expw_in, 16)
                sp.dma_start(W2[:, e], w2T[e].rearrange("(c p) n -> p c n", p=P)).then_inc(expw_in, 16)
            sp.wait_ge(pad_ok, 1)
            sp.dma_start(rows[T * P:(T + 1) * P, :], xr[:, 0, :]).then_inc(rows_out, 16)
            sp.dma_start(out[T * P:(T + 1) * P, :], xr[:, 0, 0:D]).then_inc(rows_out, 16)
            with sp.Fori(0, B) as b:
                for s in range(2):
                    at = b * S + s * HT * P
                    sp.wait_ge(x2_ok, b * 4 + (2 * s + 2))
                    sp.dma_start(out[ds(at, HT * P), :].rearrange("(t p) d -> p t d", p=P),
                                 X[:, ds(b * TB + s * HT, HT), :]).then_inc(x2_out, 16)
                    sp.wait_ge(rows_ok, b * 2 + (s + 1))
                    sp.dma_start(rows[ds(at, HT * P), :].rearrange("(t p) d -> p t d", p=P),
                                 xr[:]).then_inc(rows_out, 16)

        @block.gpsimd
        def _(pool):
            def iota(t, pattern, mult=0, start=0):
                pool.iota(t, pattern=pattern, base=start, channel_multiplier=mult,
                          allow_small_or_imprecise_dtypes=True).then_inc(iotas, 1)

            iota(iota_f[:], [[1, P]])
            iota(iota_p[:], [[0, 1]], 1)
            iota(iota_h[:], [[1, P]])
            iota(blk_h[:], [[1, BLK]])
            iota(blk_f[:], [[1, BLK]])
            iota(tok_h[:], [[P, T]], 1, 1)
            iota(k128[:], [[P, T]])
            iota(desc[:], [[-1, NK]], 0, NK)
            iota(desc_e[:], [[-1, E]], 0, E)
            iota(cum[:], [[1, E], [-1, E]])
            iota(spare[:], [[0, 1]], 1, T * P + 1)
            pool.memset(half[:], -0.5).then_inc(iotas, 1)
            pool.wait_ge(iotas, 12)
            pool.wait_ge(ln_v, 1)
            pool.tensor_tensor(rs[:], rs[:], half[:], ALU.pow).then_inc(ln_r, 1)
            with pool.Fori(0, B) as b:
                for s in range(2):
                    pool.wait_ge(v2_ok, b * 2 + (s + 1))
                    pool.tensor_tensor(rs2[:], rs2[:], half[:, 0:HT], ALU.pow).then_inc(rs2_ok, 1)

            pool.wait_ge(idx_ok, 1)
            pool.wait_ge(rows_out, 16 * (2 * B + 2))
            pool.wait_ge(x2_out, 16 * 2 * B)

            def at_rows(b):
                return bass.IndirectOffsetOnAxis(ap=idx[:, b:b + 1], axis=0)

            for b in range(BLK + GR):
                if b >= GR:
                    c = b - GR
                    pool.wait_ge(ob_ok, c + 1)
                    if c >= 1:
                        pool.wait_ge(sc_out, 16 * c)
                    pool.indirect_dma_start(out=out, out_offset=at_rows(c), in_=ob[:, c % GR, :], in_offset=None,
                                            compute_op=ALU.add).then_inc(sc_out, 16)
                if b < BLK:
                    pool.indirect_dma_start(out=xg[:, b % GR, :], out_offset=None, in_=rows, in_offset=at_rows(b)
                                            ).then_inc(g_in[b % GR], 16)
            pool.wait_ge(sc_out, 16 * BLK)

        @block.scalar
        def _(act):
            act.wait_ge(wts_in, 16 * 7)
            act.wait_ge(g_mm, 1)
            for b in range(B):
                act.copy(WGT[:, b, :, D:WG],
                         ps[:, 0, 0:2 * B * NK].rearrange("p (c b n) -> p c b n", c=DC, b=B)[:, :, b, :]
                         ).then_inc(g_out, 1)
            act.wait_ge(ks_tr, 1)
            act.copy(bd0[:], ps[:, 2, 0:4 * P].rearrange("p (b n) -> p b n", b=2 * B)[:, :, 0:NK]
                     .rearrange("p (b o) n -> p b o n", b=B)).then_inc(bd0_ok, 1)
            with act.Fori(0, B) as b:
                for t in range(TB + 2):
                    if t < TB:
                        act.wait_ge(x_tr, b * TB + (t + 1))
                        act.copy(xT[:, t % 2], ps[:, 0, 0:D].rearrange("p (c q) -> p c q", c=DC)).then_inc(xT_ok, 1)
                    if 1 <= t <= TB:
                        u = t - 1
                        act.wait_ge(q_mm, b * TB + (u + 1))
                        if u >= 2:
                            act.wait_ge(q_tr, b * 2 * TB + 2 * (u - 1))
                        act.copy(qs[:, u % 2].rearrange("p h (c w) -> p h c w", w=DH)[:, :, 0:4:3, :].bitcast(F32R),
                                 ps[:, 1 + u % 2, 0:D].rearrange("p (h w) -> p h w", w=DH).unsqueeze(2)
                                 .broadcast_to([P, H, 2, DH])).then_inc(q_hi, 1)
                    if t >= 2:
                        u = t - 2
                        act.wait_ge(q_tr, b * 2 * TB + (2 * u + 1))
                        act.copy(qT[:, 0:4, u * P:(u + 1) * P],
                                 ps[:, 3 + 2 * (u % 2), :].rearrange("p (n q) -> p n q", q=P)).then_inc(qTa_ok, 1)
                for s in range(2):
                    act.wait_ge(mx_tr, b * 2 + (s + 1))
                    act.copy(mT[:, s, :], ps[:, 7, :]).then_inc(mT_ok, 1)

                def post(s, k):
                    if k in (0, 1):
                        act.wait_ge(o_tr, b * 4 + (2 * s + k + 1))
                        act.copy(oT[:, 2 * k:2 * k + 2].rearrange("p t c q -> p (t c q)"), ps[:, 7, :]
                                 ).then_inc(oT_ok, 1)
                    if k in (5, 6):
                        act.wait_ge(x2_tr, b * 4 + (2 * s + k - 4))
                        act.copy(oT[:, 2 * (k - 5):2 * (k - 5) + 2].rearrange("p t c q -> p (t c q)"), ps[:, 7, :]
                                 ).then_inc(x2T_ok, 1)
                    if k == 8:
                        act.wait_ge(lm_ok, b * 2 + (s + 1))
                        act.activation(ex[:], lm[:], ACT.Exp).then_inc(exr_ok, 1)

                for s in range(2):
                    for p in range(NP + 2):
                        if p < NP:
                            n = s * NP + p
                            act.wait_ge(l2_mm, b * 2 * NP + (n + 1))
                            if n >= 4:
                                act.wait_ge(pv_mm, b * 2 * NG + (n // 2 - 1))
                            k = 2 * (n % 2)
                            act.activation(pT[0:NK, 2 * (n % 4):2 * (n % 4) + 2, :], ps[0:NK, k:k + 2, :], ACT.Exp
                                           ).then_inc(ex_ok, 1)
                        if s == 1:
                            post(0, p)
                for k in range(NP + 2):
                    post(1, k)

            def rows_in(b):
                act.wait_ge(gx_tr, b + 1)
                act.copy(xgT.rearrange("p c q -> p (c q)"), ps[:, 2, 0:D]).then_inc(gxT_ok, 1)

            def result(b, j, first):
                e = act.value_load(eb[0:1, ds(b, 1)], min_val=0, max_val=E - 1)
                act.wait_ge(o_mm, b + 1)
                if not first:
                    act.wait_ge(sc_out, (b - 1) * 16)
                act.activation(ob[:, j, :], ps[:, 4, 0:D], ACT.Copy, scale=xg[:, j, ds(e + D, 1)]).then_inc(ob_ok, 1)

            def step(i, first, last):
                for j in range(GR):
                    b = i * GR + j
                    act.wait_ge(h_mm, b + 1)
                    act.activation(sg, ps[:, 0, :], ACT.Silu).then_inc(sg_ok, 1)
                    if not (last and j == GR - 1):
                        rows_in(b + 1)
                    if not (first and j == 0):
                        result(b - 1, (j - 1) % GR, first)

            act.wait_ge(eb_ok, 1)
            rows_in(0)
            step(0, True, False)
            with act.Fori(1, BLK // GR - 1) as i:
                step(i, False, False)
            step(BLK // GR - 1, False, True)
            result(BLK - 1, GR - 1, False)

        @block.vector
        def _(dve):
            dve.wait_ge(iotas, 12)
            dve.tensor_scalar(ident[:], iota_f[:], iota_p[:, 0:1], None, ALU.is_equal).then_inc(consts, 1)
            dve.tensor_scalar(tri[:], iota_f[:], iota_p[:, 0:1], None, ALU.is_gt).then_inc(consts, 1)
            dve.memset(ones[:], 1.0).then_inc(consts, 1)
            dve.tensor_scalar(sel_e[:], iota_p[:], float(ONE), None, ALU.is_equal).then_inc(consts, 1)
            dve.tensor_scalar(sel_o[:], iota_p[:], float(HS + ONE), None, ALU.is_equal).then_inc(consts, 1)
            dve.tensor_scalar(neg[:], iota_f[:, 0:H], iota_p[:, 0:1], -1.0, ALU.is_equal, ALU.mult).then_inc(consts, 1)
            dve.tensor_scalar(lt8[:], cum[:], 0.0, None, ALU.is_ge).then_inc(consts, 1)
            dve.memset(ks, 0.0).then_inc(consts, 1)
            dve.memset(qs[:], 0.0).then_inc(consts, 1)
            dve.memset(on[:], 0.0).then_inc(consts, 1)
            dve.memset(vc[:], 0.0).then_inc(consts, 1)
            dve.memset(xr[:], 0.0).then_inc(pad_ok, 1)
            dve.wait_ge(consts, 11)
            dve.memset(qs[:, :, :, ONE:ONE + 1], 1.0).then_inc(consts, 1)
            for b in range(B):
                dve.wait_ge(x_in[b], 16)
                for t in range(TB):
                    dve.bn_stats(st[:, b * TB + t, :], X[:, b * TB + t, :]).then_inc(ln_st, 1)
            for t in range(T):
                if t % TB == 0:
                    dve.wait_ge(ln_st, T if t else TB)
                dve.bn_aggr(mv[:, t, :], st[:, t, :]).then_inc(ln_mv, 1)
            dve.wait_ge(ln_mv, T)
            dve.tensor_scalar(rs[:], mv[:, :, 1], EPS, None, ALU.add).then_inc(ln_v, 1)
            dve.wait_ge(kv_mm, 1)
            kv = ps[0:NK, 1, 0:B * 2 * DH].rearrange("p (b n) -> p b n", b=B)
            for b in range(B):
                for o in range(2):
                    for at in (HI_A, LO_A):
                        dve.tensor_scalar(ks[:, b, o, o * HS + at:o * HS + at + DH].bitcast(F32R),
                                          kv[:, b, 0:DH], SCALE, None, ALU.mult).then_inc(ks_hi, 1)
            dve.tensor_copy(mvb[:], kv[:, :, DH:2 * DH]).then_inc(ks_ok, 1)
            dve.wait_ge(ks_hi, 4 * B)
            for b in range(B):
                for o in range(2):
                    dve.scalar_tensor_tensor(ks[:, b, o, o * HS + HI_B:o * HS + HI_B + DH], kv[:, b, 0:DH], SCALE,
                                             ks[:, b, o, o * HS:o * HS + DH], ALU.mult, ALU.subtract
                                             ).then_inc(ks_ok, 1)
            dve.wait_ge(ln_r, 1)
            dve.wait_ge(bd0_ok, 1)
            dve.wait_ge(consts, 12)
            with dve.Fori(0, B) as b:
                for t in range(TB + 2):
                    if t < TB:
                        if t >= 2:
                            dve.wait_ge(x_tr, b * TB + (t - 1))
                        dve.tensor_scalar(xn[:, t % 2, :], X[:, ds(b * TB + t, 1), :].rearrange("p a d -> p (a d)"),
                                          mv[:, ds(b * TB + t, 1), 0], rs[:, ds(b * TB + t, 1)],
                                          ALU.subtract, ALU.mult).then_inc(xn_ok, 1)
                    if 1 <= t <= TB:
                        u = t - 1
                        dve.wait_ge(q_hi, b * TB + (u + 1))
                        qv = qs[:, u % 2]
                        dve.tensor_tensor(qv[:, :, LO_A:LO_A + DH],
                                          ps[:, 1 + u % 2, 0:D].rearrange("p (h w) -> p h w", w=DH),
                                          qv[:, :, HI_A:HI_A + DH], ALU.subtract).then_inc(q_lo, 1)
                        dve.tensor_copy(sc[:, u, :], ps[:, 1 + u % 2, D:WG]).then_inc(sc_ok, 1)
                    if t >= 2:
                        u = t - 2
                        dve.wait_ge(q_tr, b * 2 * TB + (2 * u + 2))
                        dve.tensor_copy(qT[:, 4:8, u * P:(u + 1) * P],
                                        ps[:, 4 + 2 * (u % 2), :].rearrange("p (n q) -> p n q", q=P)
                                        ).then_inc(qTb_ok, 1)
                dve.wait_ge(sc_ok, b * TB + TB)
                dve.tensor_reduce(m1[:], sc, AX.X, ALU.max).then_inc(am, 1)
                dve.wait_ge(am, b * 4 + 1)
                dve.tensor_tensor(eqw, sc, m1[:].unsqueeze(2).broadcast_to([P, TB, NK]), ALU.is_equal
                                  ).then_inc(am, 1)
                dve.wait_ge(am, b * 4 + 2)
                dve.tensor_tensor(eqw, eqw, desc[:].unsqueeze(1).broadcast_to([P, TB, NK]), ALU.mult
                                  ).then_inc(am, 1)
                dve.wait_ge(am, b * 4 + 3)
                dve.tensor_reduce(m2[:], eqw, AX.X, ALU.max).then_inc(am, 1)
                dve.wait_ge(am, b * 4 + 4)
                dve.tensor_tensor(oh, eqw, m2[:].unsqueeze(2).broadcast_to([P, TB, NK]), ALU.is_equal
                                  ).then_inc(oh_ok, 1)
                dve.wait_ge(cnt_mm, b + 1)
                dve.tensor_scalar(bias[:], ps[:, 0, 0:NK], 0.5, MASK, ALU.is_lt, ALU.mult).then_inc(cnt_ok, 1)
                dve.tensor_copy(cc[:], ps[0:NK, 7, 0:1]).then_inc(cnt_ok, 1)
                dve.wait_ge(cnt_ok, b * 2 + 2)
                for o, sel in enumerate((sel_e, sel_o)):
                    dve.scalar_tensor_tensor(bd[:, o * NK:(o + 1) * NK], bias[:], sel[:, 0:1],
                                             bd0[:, ds(b, 1), o * NK:(o + 1) * NK].rearrange("p a n -> p (a n)"),
                                             ALU.mult, ALU.add).then_inc(bd_ok, 1)
                dve.tensor_scalar(vc[:, 0:DH], mvb[:, ds(b, 1), :].rearrange("p a n -> p (a n)"), cc[:, 0:1], None,
                                  ALU.mult).then_inc(bd_ok, 1)
                dve.tensor_copy(vc[:, DH:DH + 1], cc[:]).then_inc(bd_ok, 1)
                for u in range(2 * TB):
                    t, g = divmod(u, 2)
                    k = 1 + 2 * (u % 3)
                    dve.wait_ge(l1_mm, b * 2 * TB + (u + 1))
                    dve.tensor_reduce(mx[:, t // HT, (t % HT) * H + g * 8:(t % HT) * H + g * 8 + 8],
                                      ps[:, k:k + 2, 0:4 * NK].rearrange("p k (h n) -> p k h n", n=NK),
                                      AX.X, ALU.max).then_inc(mx_ok, 1)
                def post(s, k):
                    half_b = b * 2 + s
                    here = ds(b * TB + 4 * s, HT)
                    if k in (2, 3):
                        g = k - 2
                        dve.wait_ge(wc_mm, b * 4 + (2 * s + g + 1))
                        xv = X[:, ds(b * TB + (4 * s + 2 * g), 2), :]
                        dve.tensor_tensor(xv, xv, ps[:, 7, :].rearrange("p (t d) -> p t d", d=D), ALU.add
                                          ).then_inc(x2_ok, 1)
                    if k == 3:
                        dve.wait_ge(ln_r, 1)
                        dve.wait_ge(x2_ok, b * 4 + (2 * s + 2))
                        for i in range(HT):
                            dve.bn_stats(st2[:, i, :], X[:, ds(b * TB + (4 * s + i), 1), :].rearrange("p a d -> p (a d)")
                                         ).then_inc(st2_ok, 1)
                        for i in range(HT):
                            dve.wait_ge(ln_r, 1)
                            dve.wait_ge(st2_ok, b * 8 + (4 * s + i + 1))
                            dve.bn_aggr(mv2[:, i, :], st2[:, i, :]).then_inc(mv2_ok, 1)
                        dve.wait_ge(mv2_ok, b * 8 + (4 * s + 4))
                        dve.tensor_scalar(rs2[:], mv2[:, :, 1], EPS, None, ALU.add).then_inc(v2_ok, 1)
                    if k == 4:
                        dve.wait_ge(rs2_ok, b * 2 + (s + 1))
                        dve.wait_ge(rows_out, b * 32 + (16 * s + 32))
                        for i in range(HT):
                            dve.tensor_scalar(xn2[:, i, :], X[:, ds(b * TB + (4 * s + i), 1), :].rearrange("p a d -> p (a d)"),
                                              mv2[:, i, 0:1], rs2[:, i:i + 1], ALU.subtract, ALU.mult).then_inc(xn2_ok, 1)
                    if k not in (7, 9):
                        return
                    wide = lambda a: a.unsqueeze(2).broadcast_to([P, HT, E])
                    dese = desc_e[:].unsqueeze(1).broadcast_to([P, HT, E])
                    steps = 14
                    done = [0 if k == 7 else 11]

                    def link(ins):
                        done[0] += 1
                        ins.then_inc(top, 1)
                        dve.wait_ge(top, half_b * steps + done[0])

                    if k == 7:
                        dve.wait_ge(r_mm, b * 2 + (s + 1))
                        link(dve.tensor_copy(rl[:], ps[:, 7, 0:HT * E].rearrange("p (t e) -> p t e", e=E)))
                        link(dve.tensor_reduce(r1[:], rl[:], AX.X, ALU.max))
                        dve.tensor_tensor(lm[:], rl[:], wide(r1[:]), ALU.subtract).then_inc(lm_ok, 1)
                        link(dve.tensor_tensor(eq[:], rl[:], wide(r1[:]), ALU.is_equal))
                        link(dve.tensor_tensor(eq[:], eq[:], dese, ALU.mult))
                        link(dve.tensor_reduce(f1[:], eq[:], AX.X, ALU.max))
                        link(dve.tensor_tensor(o1[:, here, :], eq[:], wide(f1[:]), ALU.is_equal))
                        link(dve.scalar_tensor_tensor(rl[:], o1[:, here, :], -1e38, rl[:], ALU.mult, ALU.add))
                        link(dve.tensor_reduce(r1[:], rl[:], AX.X, ALU.max))
                        link(dve.tensor_tensor(eq[:], rl[:], wide(r1[:]), ALU.is_equal))
                        link(dve.tensor_tensor(eq[:], eq[:], dese, ALU.mult))
                        link(dve.tensor_reduce(f1[:], eq[:], AX.X, ALU.max))
                        dve.tensor_tensor(o2[:, here, :], eq[:], wide(f1[:]), ALU.is_equal).then_inc(rl_ok, 1)
                    if k == 9:
                        dve.wait_ge(rl_ok, half_b + 1)
                        dve.tensor_tensor(cnt[:, here, :], o1[:, here, :], o2[:, here, :], ALU.add).then_inc(cnt_s, 1)
                        dve.wait_ge(exr_ok, half_b + 1)
                        link(dve.tensor_reduce(sme[:], ex[:], AX.X, ALU.add))
                        link(dve.reciprocal(sme[:], sme[:]))
                        dve.wait_ge(cnt_s, half_b + 1)
                        link(dve.tensor_tensor(ex[:], ex[:], cnt[:, here, :], ALU.mult))
                        dve.tensor_tensor(xr[:, :, D:RW], ex[:], wide(sme[:]), ALU.mult).then_inc(rows_ok, 1)

                def heads(p, s):
                    if p % 2 == 0 and p >= 2:
                        n = s * NG + p // 2 - 1
                        dve.wait_ge(pv_mm, b * 2 * NG + (n + 1))
                        if n >= 2:
                            dve.wait_ge(tu_mm, b * 2 * NG + (n - 1))
                        dve.tensor_copy(uT[:, n % 2, :], ps[:, 4 + n % 2, :]).then_inc(ut_ok, 1)
                    if p % 2 == 1 and p >= 3:
                        g = (p - 3) // 2
                        n = s * NG + g
                        dve.wait_ge(tu_mm, b * 2 * NG + (n + 1))
                        if s == 1 and g == 0:
                            dve.wait_ge(o_tr, b * 4 + 2)
                        uv = ps[:, 6, :].rearrange("p (t h w) -> p t h w", h=4, w=UH)
                        dve.reciprocal(rden[:], uv[:, :, :, DH]).then_inc(rd_ok, 1)
                        dve.wait_ge(rd_ok, b * 2 * NG + (n + 1))
                        dve.tensor_tensor(on[:].rearrange("p t (h w) -> p t h w", w=DH)[:, :, 4 * g:4 * g + 4, :],
                                          uv[:, :, :, 0:DH], rden[:].unsqueeze(3).broadcast_to([P, HT, 4, DH]), ALU.mult
                                          ).then_inc(on_ok, 1)

                for s in range(2):
                    for p in range(NP + 2):
                        heads(p, s)
                        if s == 1:
                            post(0, p)
                for k in range(NP + 2):
                    post(1, k)

            links = [0]

            def link(ins):
                links[0] += 1
                ins.then_inc(rt, 1)
                dve.wait_ge(rt, links[0])

            dve.wait_ge(pre_mm, 1)
            link(dve.tensor_tensor(ce[:], ps[:, 1, 0:E].unsqueeze(2).broadcast_to([P, E, T]),
                                   k128[:].unsqueeze(1).broadcast_to([P, E, T]), ALU.is_gt))
            link(dve.tensor_reduce(nb[:], ce[:], AX.X, ALU.add))
            link(dve.tensor_tensor(cum[:], lt8[:], nb[:].unsqueeze(1).broadcast_to([P, E, E]), ALU.mult))
            link(dve.tensor_reduce(end[:], cum[:], AX.X, ALU.add))
            link(dve.tensor_tensor(base[:], end[:], nb[:], ALU.subtract))
            link(dve.tensor_scalar(base[:], base[:], float(P), None, ALU.mult))
            link(dve.tensor_tensor(slf[:], ps[:, 0, 0:T * E].rearrange("p (t e) -> p t e", e=E),
                                   base[:].unsqueeze(1).broadcast_to([P, T, E]), ALU.add))
            for k, o in enumerate((o1, o2)):
                link(dve.tensor_tensor(pick[:], slf[:], o[:], ALU.mult))
                link(dve.tensor_reduce(slot[:, k, :], pick[:], AX.X, ALU.add))
            link(dve.tensor_copy(sloti[:], slot[:].rearrange("p k t -> p (k t)")))
            link(dve.tensor_scalar(bki[:], sloti[:], 7, None, ALU.logical_shift_right))
            link(dve.tensor_scalar(rmi[:], sloti[:], P - 1, None, ALU.bitwise_and))
            link(dve.tensor_copy(bkh[:], bki[:]))
            link(dve.tensor_copy(rmf[:], rmi[:]))
            link(dve.tensor_tensor(bsel, blk_h[:].unsqueeze(1).broadcast_to([P, 2 * T, BLK]),
                                   bkh[:].unsqueeze(2).broadcast_to([P, 2 * T, BLK]), ALU.is_equal))
            for k in range(2):
                link(dve.tensor_tensor(bval[:, k * T:(k + 1) * T, :], bsel[:, k * T:(k + 1) * T, :],
                                       tok_h[:].unsqueeze(2).broadcast_to([P, T, BLK]), ALU.mult))

            def spread(i, first):
                for j in range(4):
                    if not first:
                        dve.wait_ge(asel_used, i * 4 + (j - 3))
                    dve.tensor_scalar(asel[:, j, :], iota_h[:], rmf[:, ds(i * 4 + j, 1)], None, ALU.is_equal
                                      ).then_inc(asel_ok, 1)

            spread(0, True)
            with dve.Fori(1, 2 * T // 4) as i:
                spread(i, False)
            link(dve.tensor_tensor(ebc, blk_f[:].unsqueeze(2).broadcast_to([P, BLK, E]),
                                   end[:].unsqueeze(1).broadcast_to([P, BLK, E]), ALU.is_ge))
            link(dve.tensor_reduce(ebf[:], ebc, AX.X, ALU.add))
            dve.tensor_scalar(eb[:], ebf[:], float(E - 1), None, ALU.min).then_inc(eb_ok, 1)
            dve.wait_ge(asel_used, 2 * T)
            link(dve.tensor_copy(tokp[:], ps[:, 2, 0:BLK]))
            link(dve.tensor_scalar(idf[:], tokp[:], 0.0, spare[:, 0:1], ALU.is_equal, ALU.mult))
            dve.scalar_tensor_tensor(idx[:], tokp[:], -1.0, idf[:], ALU.add, ALU.add).then_inc(idx_ok, 1)

            def step(i):
                for j in range(GR):
                    b = i * GR + j
                    dve.wait_ge(sg_ok, b + 1)
                    dve.tensor_tensor(yb, sg, ps[:, 1, :], ALU.mult).then_inc(y_ok, 1)
                    dve.wait_ge(y_tr, b + 1)
                    dve.tensor_copy(yT[:].rearrange("p c q -> p (c q)"), ps[:, 3, :]).then_inc(yT_ok, 1)

            with dve.Fori(0, BLK // GR) as i:
                step(i)

        @block.tensor
        def _(pe):
            pe.wait_ge(wts_in, 16 * 7)
            for c in range(DC):
                for k in range(DC):
                    mm = pe.matmul(ps[:, 0, c * B * NK:(c + 1) * B * NK], WQ[:, k, c * P:(c + 1) * P], CT[:, k, :],
                                   start=(k == 0), stop=(k == DC - 1))
            mm.then_inc(g_mm, 1)
            for b in range(B):
                for k in range(DC):
                    mm = pe.matmul(ps[0:NK, 1, b * 2 * DH:(b + 1) * 2 * DH], CT[:, k, b * NK:(b + 1) * NK], WKV[:, k, :],
                                   start=(k == 0), stop=(k == DC - 1))
            mm.then_inc(kv_mm, 1)
            pe.wait_ge(consts, 12)
            pe.wait_ge(ks_ok, 2 * B + 1)
            for n in range(2 * B):
                mm = pe.transpose(ps[:, 2, n * P:n * P + NK], ks[:, n // 2, n % 2, :], ident[0:NK, 0:NK])
            mm.then_inc(ks_tr, 1)
            pe.wait_ge(g_out, B)
            pe.wait_ge(bd0_ok, 1)
            with pe.Fori(0, B) as b:
                def turn_x(t):
                    pe.wait_ge(xn_ok, b * TB + (t + 1))
                    for c in range(DC):
                        mm = pe.transpose(ps[:, 0, c * P:(c + 1) * P], xn[:, t % 2, c * P:(c + 1) * P], ident[:])
                    mm.then_inc(x_tr, 1)

                def project(t):
                    pe.wait_ge(xT_ok, b * TB + (t + 1))
                    if t >= 2:
                        pe.wait_ge(sc_ok, b * TB + (t - 1))
                    for c in range(DC):
                        mm = pe.matmul(ps[:, 1 + t % 2, 0:WG], xT[:, t % 2, c, :],
                                       WGT[:, ds(b, 1), c, :].rearrange("p a n -> p (a n)"),
                                       start=(c == 0), stop=(c == DC - 1))
                    mm.then_inc(q_mm, 1)

                def turn_q(t):
                    pe.wait_ge(q_lo, b * TB + (t + 1))
                    if t >= 2:
                        pe.wait_ge(qTa_ok, b * TB + (t - 1))
                        pe.wait_ge(qTb_ok, b * TB + (t - 1))
                    for g in range(2):
                        for n in range(4):
                            a = 2 * (4 * g + n)
                            mm = pe.transpose(ps[:, 3 + 2 * (t % 2) + g, n * P:(n + 1) * P],
                                              qs[:, t % 2, a:a + 2, :].rearrange("p h w -> p (h w)"), ident[:])
                        mm.then_inc(q_tr, 1)

                turn_x(0)
                for t in range(TB):
                    project(t)
                    if t + 1 < TB:
                        turn_x(t + 1)
                    if t >= 1:
                        turn_q(t - 1)
                turn_q(TB - 1)
                pe.wait_ge(oh_ok, b + 1)
                for t in range(TB):
                    pe.matmul(ps[:, 0, 0:NK], ones[:], oh[:, t, :], start=(t == 0), stop=(t == TB - 1))
                for t in range(TB):
                    mm = pe.matmul(ps[0:NK, 7, 0:1], oh[:, t, :], ones[:, 0:1], start=(t == 0), stop=(t == TB - 1))
                mm.then_inc(cnt_mm, 1)
                pe.wait_ge(bd_ok, b * 4 + 4)
                pe.wait_ge(qTa_ok, b * TB + TB)
                pe.wait_ge(qTb_ok, b * TB + TB)
                for u in range(2 * TB):
                    t, g = divmod(u, 2)
                    k = 1 + 2 * (u % 3)
                    if u >= 3:
                        pe.wait_ge(mx_ok, b * 2 * TB + (u - 2))
                    for n in range(4):
                        mm = pe.matmul(ps[:, k + n // 2, (n % 2) * 2 * NK:(n % 2 + 1) * 2 * NK],
                                       qT[:, 4 * g + n, t * P:(t + 1) * P], bd[:], start=True, stop=True)
                    mm.then_inc(l1_mm, 1)
                for s in range(2):
                    pe.wait_ge(mx_ok, b * 2 * TB + (TB * (s + 1)))
                    if s == 1:
                        pe.wait_ge(mT_ok, b * 2 + 1)
                    for i in range(HT):
                        mm = pe.transpose(ps[:, 7, i * P:(i + 1) * P], mx[:, s, i * H:i * H + P], ident[:])
                    mm.then_inc(mx_tr, 1)
                pe.wait_ge(mx_ok, b * 2 * TB + 2 * TB)

                def logits(n):
                    s, p = divmod(n, NP)
                    if n >= 2:
                        pe.wait_ge(ex_ok, b * 2 * NP + (n - 1))
                    for o in range(2):
                        k = 2 * (n % 2) + o
                        pe.matmul(ps[0:NK, k, :], bd[:, o * NK:(o + 1) * NK],
                                  qT[:, p, s * 512:(s + 1) * 512], start=True, stop=False)
                        mm = pe.matmul(ps[0:NK, k, :], neg[:, 2 * p + o:2 * p + o + 1].broadcast_to([P, NK]), mT[:, s, :],
                                       start=False, stop=True)
                    mm.then_inc(l2_mm, 1)

                def sums(n):
                    pe.wait_ge(ex_ok, b * 2 * NP + (2 * n + 2))
                    for h in range(4):
                        mm = pe.matmul(ps[h * UH:(h + 1) * UH, 4 + n % 2, :], vc[:], pT[0:NK, 4 * (n % 2) + h, :],
                                       start=True, stop=True)
                    mm.then_inc(pv_mm, 1)

                def turn_sums(n):
                    pe.wait_ge(ut_ok, b * 2 * NG + (n + 1))
                    if n >= 1:
                        pe.wait_ge(on_ok, b * 2 * NG + n)
                    for i in range(HT):
                        mm = pe.transpose(ps[:, 6, i * P:(i + 1) * P], uT[:, n % 2, i * P:(i + 1) * P], ident[:])
                    mm.then_inc(tu_mm, 1)

                def turn(src, g, done):
                    for i in range(2 * g, 2 * g + 2):
                        for c in range(DC):
                            mm = pe.transpose(ps[:, 7, ((i % 2) * DC + c) * P:((i % 2) * DC + c + 1) * P],
                                              src[:, i, c * P:(c + 1) * P], ident[:])
                    mm.then_inc(done, 1)

                def post(s, k):
                    if k == 0:
                        pe.wait_ge(on_ok, b * 2 * NG + (NG * (s + 1)))
                        turn(on, 0, o_tr)
                    if k == 1:
                        pe.wait_ge(oT_ok, b * 4 + (2 * s + 1))
                        turn(on, 1, o_tr)
                    if k in (2, 3):
                        g = k - 2
                        pe.wait_ge(oT_ok, b * 4 + (2 * s + 2))
                        if g:
                            pe.wait_ge(x2_ok, b * 4 + (2 * s + 1))
                        for i in range(2 * g, 2 * g + 2):
                            for c in range(DC):
                                mm = pe.matmul(ps[:, 7, (i % 2) * D:(i % 2 + 1) * D], oT[:, i, c, :], WC[:, c, :],
                                               start=(c == 0), stop=(c == DC - 1))
                        mm.then_inc(wc_mm, 1)
                    if k == 5:
                        pe.wait_ge(xn2_ok, b * 8 + (4 * s + 4))
                        turn(xn2, 0, x2_tr)
                    if k == 6:
                        pe.wait_ge(x2T_ok, b * 4 + (2 * s + 1))
                        turn(xn2, 1, x2_tr)
                    if k == 7:
                        pe.wait_ge(x2T_ok, b * 4 + (2 * s + 2))
                        for i in range(HT):
                            for c in range(DC):
                                mm = pe.matmul(ps[:, 7, i * E:(i + 1) * E], oT[:, i, c, :], RT[:, c, :],
                                               start=(c == 0), stop=(c == DC - 1))
                        mm.then_inc(r_mm, 1)

                for s in range(2):
                    pe.wait_ge(mT_ok, b * 2 + (s + 1))
                    for p in range(NP + 2):
                        if p < NP:
                            logits(s * NP + p)
                        if p % 2 == 0 and p >= 2:
                            sums(s * NG + p // 2 - 1)
                        if p % 2 == 1 and p >= 3:
                            turn_sums(s * NG + (p - 3) // 2)
                        if s == 1:
                            post(0, p)
                for k in range(NP + 2):
                    post(1, k)
                pe.wait_ge(rl_ok, b * 2 + 2)

            pe.wait_ge(cnt_s, 2 * B)
            pe.matmul(ps[:, 0, 0:T * E], tri[:], cnt[:].rearrange("p t e -> p (t e)"), start=True, stop=False)
            for t in range(T - 1):
                pe.matmul(ps[:, 0, (t + 1) * E:T * E].rearrange("p (t e) -> p t e", e=E), ones[:],
                          cnt[:, t, :].unsqueeze(1).broadcast_to([P, T - 1 - t, E]), start=False, stop=(t == T - 2))
            for t in range(T):
                mm = pe.matmul(ps[:, 1, 0:E], ones[:], cnt[:, t, :], start=(t == 0), stop=(t == T - 1))
            mm.then_inc(pre_mm, 1)
            for n in range(2 * T):
                pe.wait_ge(asel_ok, n + 1)
                pe.matmul(ps[:, 2, 0:BLK], asel[:, n % 4, :], bval[:, n, :], start=(n == 0), stop=(n == 2 * T - 1)
                          ).then_inc(asel_used, 1)

            pe.wait_ge(expw_in, 16 * 2 * E)
            pe.wait_ge(eb_ok, 1)
            pe.wait_ge(idx_ok, 1)

            def turn_rows(j, value):
                pe.wait_ge(g_in[j], value)
                for c in range(DC):
                    mm = pe.transpose(ps[:, 2, c * P:(c + 1) * P], xg[:, j, c * P:(c + 1) * P], ident[:])
                mm.then_inc(gx_tr, 1)

            def inner(b, e):
                pe.wait_ge(gxT_ok, b + 1)
                for f in range(2):
                    for c in range(DC):
                        mm = pe.matmul(ps[:, f, :], xgT[:, c, :],
                                       W1[:, ds(e, 1), c, f * FI:(f + 1) * FI].rearrange("p a n -> p (a n)"),
                                       start=(c == 0), stop=(c == DC - 1))
                mm.then_inc(h_mm, 1)

            def outer(b, e):
                pe.wait_ge(yT_ok, b + 1)
                for c in range(FC):
                    mm = pe.matmul(ps[:, 4, 0:D], yT[:, c, :], W2[:, ds(e, 1), c, :].rearrange("p a n -> p (a n)"),
                                   start=(c == 0), stop=(c == FC - 1))
                mm.then_inc(o_mm, 1)

            def turn_y(b):
                pe.wait_ge(y_ok, b + 1)
                for c in range(FC):
                    mm = pe.transpose(ps[:, 3, c * P:(c + 1) * P], yb[:, c * P:(c + 1) * P], ident[:])
                mm.then_inc(y_tr, 1)

            def expert(b):
                return pe.value_load(eb[0:1, ds(b, 1)], min_val=0, max_val=E - 1)

            def step(i, first, last):
                for j in range(GR):
                    b = i * GR + j
                    inner(b, expert(b))
                    if not (last and j == GR - 1):
                        turn_rows((j + 1) % GR, i * 16 + (16 if j < GR - 1 else 32))
                    if not (first and j == 0):
                        e = expert(b - 1)
                        if not (first and j == 1):
                            pe.wait_ge(ob_ok, b - 1)
                        outer(b - 1, e)
                    turn_y(b)

            turn_rows(0, 16)
            step(0, True, False)
            with pe.Fori(1, BLK // GR - 1) as i:
                step(i, False, False)
            step(BLK // GR - 1, False, True)
            e = expert(BLK - 1)
            pe.wait_ge(ob_ok, BLK - 1)
            outer(BLK - 1, e)


def kernel(x, ctx_1024, L0_xattn_Wq, L0_xattn_Wkv, L0_xattn_Wc, L0_ffn_w1, L0_ffn_w2, L0_ffn_router_w):
    import numpy as np
    from concourse import bacc
    from concourse.bass_utils import run_bass_kernel_spmd

    nc = bacc.Bacc("TRN2", target_bir_lowering=False, num_devices=1)
    laid = {
        "x": np.asarray(x).reshape(B * S, D),
        "ctxT": np.asarray(ctx_1024).reshape(B * NK, D).T,
        "Wq": np.asarray(L0_xattn_Wq),
        "WqT": np.asarray(L0_xattn_Wq).T,
        "WkvT": np.asarray(L0_xattn_Wkv).T,
        "WcT": np.asarray(L0_xattn_Wc).T,
        "routerT": np.asarray(L0_ffn_router_w).T,
        "w1T": np.asarray(L0_ffn_w1).transpose(0, 2, 1),
        "w2T": np.asarray(L0_ffn_w2).transpose(0, 2, 1),
    }
    arrays, args = {}, {}
    for name, a in laid.items():
        arrays[f"in_{name}"] = np.ascontiguousarray(a)
        args[name] = nc.dram_tensor(f"in_{name}", a.shape, mybir.dt.from_np(a.dtype), kind="ExternalInput").ap()
    args["out"] = nc.dram_tensor("out_x", [B * S + P, D], F32, kind="ExternalOutput").ap()
    build(nc, **args)
    r = run_bass_kernel_spmd(nc, [arrays], core_ids=[0])
    return r.results[0]["out_x"][0:B * S].reshape(B, S, D)
```

```python
from contextlib import ExitStack

import concourse.bass as bass
from concourse import mybir

F32 = mybir.dt.float32
F32R = mybir.dt.float32r
F16 = mybir.dt.float16
BF16 = mybir.dt.bfloat16
I32 = mybir.dt.int32
U32 = mybir.dt.uint32
ALU = mybir.AluOpType
ACT = mybir.ActivationFunctionType
AX = mybir.AxisListType
ds = bass.ds

P = 128
D = 256
DC = D // P
B = 2
S = 1024
TB = S // P
T = B * TB
HT = TB // 2
NH = T // HT
NK = 77
H = 16
DH = D // H
NP = H // 2
HS = P // 2
UH = 32
NG = H // 4
RW = D + 8
E = 8
FI = 512
FC = FI // P
BLK = 2 * S * B // P + E - 1
GR = 4
LAST = (BLK - 1) // GR
SCALE = 0.25
MASK = -1e30
EPS = 1e-5
assert HT >= GR and DH ** -0.5 == SCALE

SLOTS = NP + 2
XN_AT = (0, 0, 2, 4)
X_AT = (0, 1, 3, 5)
P_AT = (0, 2, 4, 6)
SCORES_AT = (1, 2, 3, 4)
PICKS_AT = 5
MASKS_AT = (1, 8)

HI_A, LO_A, ONE, HI_B = 0, DH, 2 * DH, 3 * DH


def build(nc, x, ctxT, Wq, WqT, WkvT, WcT, routerT, w1T, w2T, out):
    rows = nc.dram_tensor("rows", [(T + 1) * P, RW], F32).ap()
    with ExitStack() as ctx:
        def sb(name, shape, dt=F32):
            return ctx.enter_context(nc.sbuf_tensor(name, shape, dt))

        def sem(name):
            return ctx.enter_context(nc.semaphore(name))

        ps = ctx.enter_context(nc.psum_tensor("ps", [P, 8, 512], F32))

        iota_f = sb("iota_f", [P, P])
        iota_p = sb("iota_p", [P, 1])
        iota_h = sb("iota_h", [P, P], F16)
        blk_h = sb("blk_h", [P, BLK], F16)
        blk_f = sb("blk_f", [P, BLK])
        tok_h = sb("tok_h", [P, T], F16)
        spare = sb("spare", [P, 1])
        k128 = sb("k128", [P, T])
        desc = sb("desc", [P, NK], BF16)
        desc_e = sb("desc_e", [P, E])
        lt8 = sb("lt8", [P, E, E])
        ident = sb("ident", [P, P])
        tri = sb("tri", [P, P], BF16)
        ones = sb("ones", [P, P], BF16)
        sel_e = sb("sel_e", [P, 1])
        sel_o = sb("sel_o", [P, 1])
        neg = sb("neg", [P, H], F32R)
        half = sb("half", [P, T])
        X = sb("X", [P, T, D])
        WQT = sb("WQT", [P, DC, D])
        GT = sb("GT", [P, DC, B, NK])
        WKV = sb("WKV", [P, DC, 2 * DH])
        WC = sb("WC", [P, DC, D])
        RT = sb("RT", [P, DC, E])
        mvb = sb("mvb", [NK, B, DH])
        bd = sb("bd", [P, B, 2 * NK], F32R)
        vc = sb("vc", [NK, B, UH])
        cc = sb("cc", [NK, B])
        bias = sb("bias", [P, B, NK])
        st = sb("st", [P, T, 6])
        mv = sb("mv", [P, T, 2])
        rs = sb("rs", [P, T])
        xp = sb("xp", [P, 2, D])
        xpT = sb("xpT", [P, 2, DC, P])
        qs = sb("qs", [P, H, HS])
        qT = sb("qT", [P, 2, NP, HT * P], F32R)
        m1 = sb("m1", [P, T])
        m2 = sb("m2", [P, T])
        mx = sb("mx", [P, (HT - 1) * H + P])
        mT = sb("mT", [P, HT * P], F32R)
        pT = sb("pT", [P, 8, 512])
        uT = sb("uT", [P, 2, 512])
        rden = sb("rden", [P, HT, 4])
        on = sb("on", [P, HT, D])
        oT = sb("oT", [P, HT, DC, P])
        st2 = sb("st2", [P, HT, 6])
        mv2 = sb("mv2", [P, HT, 2])
        rs2 = sb("rs2", [P, HT])
        xr = sb("xr", [P, HT, RW])
        xn2 = xr[:, :, 0:D]
        rl = sb("rl", [P, HT, E])
        r1 = sb("r1", [P, HT])
        f1 = sb("f1", [P, HT])
        eq = sb("eq", [P, HT, E])
        lm = sb("lm", [P, HT, E])
        ex = sb("ex", [P, HT, E])
        sme = sb("sme", [P, HT])
        o1 = sb("o1", [P, T, E])
        o2 = sb("o2", [P, T, E])
        cnt = sb("cnt", [P, T, E], BF16)
        ce = sb("ce", [P, E, T])
        nb = sb("nb", [P, E])
        cum = sb("cum", [P, E, E])
        end = sb("end", [P, E])
        base = sb("base", [P, E])
        slf = sb("slf", [P, T, E])
        pick = sb("pick", [P, T, E])
        slot = sb("slot", [P, 2, T])
        sloti = sb("sloti", [P, 2 * T], I32)
        bki = sb("bki", [P, 2 * T], I32)
        rmi = sb("rmi", [P, 2 * T], I32)
        bkh = sb("bkh", [P, 2 * T], F16)
        rmh = sb("rmh", [P, 2 * T], F16)
        ebf = sb("ebf", [P, BLK])
        eb = sb("eb", [P, BLK], I32)
        tokp = sb("tokp", [P, BLK])
        idf = sb("idf", [P, BLK])
        idx = sb("idx", [P, BLK], U32)
        W1 = sb("W1", [P, E, DC, 2 * FI])
        W2 = sb("W2", [P, E, FC, D])
        pT1 = pT[:].rearrange("p n q -> p (n q)")
        ns = T * NK
        sc = pT1[:, 0:ns].rearrange("p (t n) -> p t n", n=NK)
        eqw = pT1[:, ns:3 * ns // 2].bitcast(BF16).rearrange("p (t n) -> p t n", n=NK)
        oh = pT1[:, 3 * ns // 2:2 * ns].bitcast(BF16).rearrange("p (t n) -> p t n", n=NK)
        bd0 = pT1[:, 2 * ns:2 * ns + 2 * B * NK].rearrange("p (b n) -> p b n", b=B)
        nh = 2 * T * BLK // 2
        bsel = pT1[:, 0:nh].bitcast(F16).rearrange("p (t b) -> p t b", b=BLK)
        bval = pT1[:, nh:2 * nh].bitcast(F16).rearrange("p (t b) -> p t b", b=BLK)
        ebc = pT1[:, 2 * nh:2 * nh + BLK * E].rearrange("p (b e) -> p b e", e=E)
        asel = pT1[:, 2 * nh + BLK * E:2 * nh + BLK * E + T * P].bitcast(F16).rearrange("p (n q) -> p n q", q=P)
        yT = pT1[:, 0:FI].rearrange("p (c q) -> p c q", c=FC)
        xn = on
        xT = oT
        ks = oT[0:NK, 2:4].rearrange("p t c q -> p (t c q)").rearrange("p (b o n) -> p b o n", b=B, o=2)
        qs1 = qs[:].rearrange("p h w -> p (h w)")
        xg = xr
        xgT = qs1[:, 0:D].rearrange("p (c q) -> p c q", c=DC)
        sg = uT[:, 0, :]
        yb = uT[:, 1, :]
        ob = oT[:].rearrange("p t c q -> p t (c q)")
        uT1 = uT[:].rearrange("p a b -> p (a b)")
        WQ = uT1[:, 0:DC * D].rearrange("p (c n) -> p c n", c=DC)
        CT = uT1[:, DC * D:DC * (D + B * NK)].rearrange("p (c n) -> p c n", c=DC)

        x_in = [sem(f"x_in{i}") for i in range(B)]
        wts_in = sem("wts_in")
        expw_in = sem("expw_in")
        iotas = sem("iotas")
        consts = sem("consts")
        ln_st = sem("ln_st")
        ln_mv = sem("ln_mv")
        ln_v = sem("ln_v")
        ln_r = sem("ln_r")
        g_mm = sem("g_mm")
        g_out = sem("g_out")
        kv_mm = sem("kv_mm")
        ks_hi = sem("ks_hi")
        ks_ok = sem("ks_ok")
        ks_tr = sem("ks_tr")
        bd0_ok = sem("bd0_ok")
        xn_ok = sem("xn_ok")
        xp_ok = sem("xp_ok")
        x_tr = sem("x_tr")
        xT_ok = sem("xT_ok")
        px_tr = sem("px_tr")
        pxT_ok = sem("pxT_ok")
        q_mm = sem("q_mm")
        q_sc = sem("q_sc")
        q_hi = sem("q_hi")
        q_lo = sem("q_lo")
        sc_ok = sem("sc_ok")
        q_tr = sem("q_tr")
        qT_ok = sem("qT_ok")
        am = sem("am")
        oh_ok = sem("oh_ok")
        cnt_mm = sem("cnt_mm")
        cnt_ok = sem("cnt_ok")
        bd_ok = sem("bd_ok")
        l1_mm = sem("l1_mm")
        mx_ok = sem("mx_ok")
        mx_tr = sem("mx_tr")
        mT_ok = sem("mT_ok")
        l2_mm = sem("l2_mm")
        ex_ok = sem("ex_ok")
        pv_mm = sem("pv_mm")
        ut_ok = sem("ut_ok")
        tu_mm = sem("tu_mm")
        rd_ok = sem("rd_ok")
        on_ok = sem("on_ok")
        o_tr = sem("o_tr")
        oT_ok = sem("oT_ok")
        wc_mm = sem("wc_mm")
        x2_ok = sem("x2_ok")
        st2_ok = sem("st2_ok")
        mv2_ok = sem("mv2_ok")
        v2_ok = sem("v2_ok")
        rs2_ok = sem("rs2_ok")
        xn2_ok = sem("xn2_ok")
        rows_ok = sem("rows_ok")
        rows_out = sem("rows_out")
        x2_out = sem("x2_out")
        x2_tr = sem("x2_tr")
        x2T_ok = sem("x2T_ok")
        r_mm = sem("r_mm")
        top = sem("top")
        cnt_s = sem("cnt_s")
        rl_ok = sem("rl_ok")
        rt = sem("rt")
        lm_ok = sem("lm_ok")
        exr_ok = sem("exr_ok")
        pad_ok = sem("pad_ok")
        pre_mm = sem("pre_mm")
        asel_ok = sem("asel_ok")
        asel_used = sem("asel_used")
        idx_ok = sem("idx_ok")
        eb_ok = sem("eb_ok")
        g_in = [sem(f"g_in{j}") for j in range(GR)]
        gx_tr = sem("gx_tr")
        gxT_ok = sem("gxT_ok")
        h_mm = sem("h_mm")
        sg_ok = sem("sg_ok")
        y_ok = sem("y_ok")
        y_tr = sem("y_tr")
        yT_ok = sem("yT_ok")
        o_mm = sem("o_mm")
        ob_ok = sem("ob_ok")
        sc_out = sem("sc_out")

        block = ctx.enter_context(nc.Block())

        @block.sync
        def _(sp):
            sp.dma_start(X[:, 0:TB, :], x[0:S, :].rearrange("(t p) d -> p t d", p=P)).then_inc(x_in[0], 16)
            sp.dma_start(CT, ctxT.rearrange("(c p) n -> p c n", p=P)).then_inc(wts_in, 16)
            sp.dma_start(WQ[:], Wq.rearrange("(c p) n -> p c n", p=P)).then_inc(wts_in, 16)
            sp.dma_start(WKV[:], WkvT.rearrange("(c p) n -> p c n", p=P)).then_inc(wts_in, 16)
            sp.dma_start(WQT[:], WqT.rearrange("(c p) n -> p c n", p=P)).then_inc(wts_in, 16)
            sp.dma_start(WC[:], WcT.rearrange("(c p) n -> p c n", p=P)).then_inc(wts_in, 16)
            sp.dma_start(RT[:], routerT.rearrange("(c p) n -> p c n", p=P)).then_inc(wts_in, 16)
            sp.dma_start(X[:, TB:T, :], x[S:2 * S, :].rearrange("(t p) d -> p t d", p=P)).then_inc(x_in[1], 16)
            for e in range(E):
                sp.dma_start(W1[:, e], w1T[e].rearrange("(c p) n -> p c n", p=P)).then_inc(expw_in, 16)
                sp.dma_start(W2[:, e], w2T[e].rearrange("(c p) n -> p c n", p=P)).then_inc(expw_in, 16)
            sp.wait_ge(pad_ok, 1)
            sp.dma_start(rows[T * P:(T + 1) * P, :], xr[:, 0, :]).then_inc(rows_out, 16)
            sp.dma_start(out[T * P:(T + 1) * P, :], xr[:, 0, 0:D]).then_inc(rows_out, 16)
            with sp.Fori(0, B) as b:
                for s in range(2):
                    at = b * S + s * HT * P
                    sp.wait_ge(x2_ok, b * 4 + (2 * s + 2))
                    sp.dma_start(out[ds(at, HT * P), :].rearrange("(t p) d -> p t d", p=P),
                                 X[:, ds(b * TB + s * HT, HT), :]).then_inc(x2_out, 16)
                    sp.wait_ge(rows_ok, b * 2 + (s + 1))
                    sp.dma_start(rows[ds(at, HT * P), :].rearrange("(t p) d -> p t d", p=P),
                                 xr[:]).then_inc(rows_out, 16)

        @block.gpsimd
        def _(pool):
            def iota(t, pattern, mult=0, start=0):
                pool.iota(t, pattern=pattern, base=start, channel_multiplier=mult,
                          allow_small_or_imprecise_dtypes=True).then_inc(iotas, 1)

            iota(iota_f[:], [[1, P]])
            iota(iota_p[:], [[0, 1]], 1)
            iota(iota_h[:], [[1, P]])
            iota(blk_h[:], [[1, BLK]])
            iota(blk_f[:], [[1, BLK]])
            iota(tok_h[:], [[P, T]], 1, 1)
            iota(k128[:], [[P, T]])
            iota(desc[:], [[-1, NK]], 0, NK)
            iota(desc_e[:], [[-1, E]], 0, E)
            iota(cum[:], [[1, E], [-1, E]])
            iota(spare[:], [[0, 1]], 1, T * P + 1)
            pool.memset(half[:], -0.5).then_inc(iotas, 1)
            pool.wait_ge(iotas, 12)
            for b in range(B):
                pool.wait_ge(ln_v, b + 1)
                pool.tensor_tensor(rs[:, b * TB:(b + 1) * TB], rs[:, b * TB:(b + 1) * TB], half[:, 0:TB], ALU.pow
                                   ).then_inc(ln_r, 1)
            with pool.Fori(0, NH) as v:
                pool.wait_ge(v2_ok, v + 1)
                pool.tensor_tensor(rs2[:], rs2[:], half[:, 0:HT], ALU.pow).then_inc(rs2_ok, 1)

            pool.wait_ge(idx_ok, 1)
            pool.wait_ge(rows_out, 16 * (2 * B + 2))
            pool.wait_ge(x2_out, 16 * 2 * B)

            def at_rows(b):
                return bass.IndirectOffsetOnAxis(ap=idx[:, b:b + 1], axis=0)

            for b in range(BLK + GR):
                if b >= GR:
                    c = b - GR
                    pool.wait_ge(ob_ok, c + 1)
                    if c >= 1:
                        pool.wait_ge(sc_out, 16 * c)
                    pool.indirect_dma_start(out=out, out_offset=at_rows(c), in_=ob[:, c % GR, :], in_offset=None,
                                            compute_op=ALU.add).then_inc(sc_out, 16)
                if b < BLK:
                    pool.indirect_dma_start(out=xg[:, b % GR, :], out_offset=None, in_=rows, in_offset=at_rows(b)
                                            ).then_inc(g_in[b % GR], 16)
            pool.wait_ge(sc_out, 16 * BLK)

        @block.scalar
        def _(act):
            act.wait_ge(wts_in, 16 * 6)
            act.wait_ge(g_mm, 1)
            act.copy(GT[:], ps[:, 0, 0:2 * B * NK].rearrange("p (c b n) -> p c b n", c=DC, b=B)).then_inc(g_out, 1)
            act.wait_ge(ks_tr, 1)
            act.copy(bd0.rearrange("p b (o n) -> p b o n", o=2),
                     ps[:, 2, 0:4 * P].rearrange("p (b n) -> p b n", b=2 * B)[:, :, 0:NK]
                     .rearrange("p (b o) n -> p b o n", b=B)).then_inc(bd0_ok, 1)

            def score_rows(b, j):
                n = b * HT + j
                act.wait_ge(x_tr, n + 1)
                i = 2 * (j % 2)
                act.copy(xT[:, i:i + 2], ps[:, j % 2, :].rearrange("p (t c q) -> p t c q", t=2, c=DC)).then_inc(xT_ok, 1)

            def exps(u, p):
                n = u * NP + p
                act.wait_ge(l2_mm, n + 1)
                if n >= 4:
                    act.wait_ge(pv_mm, (n - 4) // 2 + 1)
                act.activation(pT[0:NK, 2 * (n % 4):2 * (n % 4) + 2, :], ps[0:NK, 0:2, :], ACT.Exp).then_inc(ex_ok, 1)

            def prep_turned(w, z):
                t, g = divmod(z, 2)
                act.wait_ge(q_tr, w * 2 * HT + z + 1)
                act.copy(qT[:, w % 2, 4 * g:4 * g + 4, t * P:(t + 1) * P],
                         ps[:, 5, :].rearrange("p (n q) -> p n q", q=P)).then_inc(qT_ok, 1)

            def prep(w, p):
                if p in X_AT:
                    t = X_AT.index(p)
                    act.wait_ge(px_tr, w * HT + t + 1)
                    act.copy(xpT[:, t % 2], ps[:, 4, 0:D].rearrange("p (c q) -> p c q", c=DC)).then_inc(pxT_ok, 1)
                if p in P_AT:
                    q = w * HT + P_AT.index(p)
                    act.wait_ge(q_mm, q + 1)
                    if q:
                        act.wait_ge(q_tr, 2 * q)
                    act.copy(qs[:].rearrange("p h (c w) -> p h c w", w=DH)[:, :, 0:4:3, :].bitcast(F32R),
                             ps[:, 4, 0:D].rearrange("p (h w) -> p h w", w=DH).unsqueeze(2)
                             .broadcast_to([P, H, 2, DH])).then_inc(q_hi, 1)

            def post(v, k):
                if k in (0, 1):
                    act.wait_ge(o_tr, 2 * v + k + 1)
                    act.copy(oT[:, 2 * k:2 * k + 2].rearrange("p t c q -> p (t c q)"), ps[:, 3, :]).then_inc(oT_ok, 1)
                if k in (5, 6):
                    act.wait_ge(x2_tr, 2 * v + k - 4)
                    act.copy(oT[:, 2 * (k - 5):2 * (k - 5) + 2].rearrange("p t c q -> p (t c q)"), ps[:, 3, :]
                             ).then_inc(x2T_ok, 1)
                if k == 8:
                    act.wait_ge(lm_ok, v + 1)
                    act.activation(ex[:], lm[:], ACT.Exp).then_inc(exr_ok, 1)

            for j in range(HT):
                score_rows(0, j)
            for u in range(-1, NH + 1):
                for p in range(SLOTS):
                    if u + 1 < NH and 1 <= p <= 2 * HT:
                        prep_turned(u + 1, p - 1)
                    if 0 <= u < NH and 1 <= p <= NP:
                        exps(u, p - 1)
                    if u + 1 < NH:
                        prep(u + 1, p)
                    if u < 0 and p in SCORES_AT:
                        score_rows(1, SCORES_AT.index(p))
                    if u >= 1 and p:
                        post(u - 1, p - 1)
                if u + 1 < NH:
                    act.wait_ge(mx_tr, u + 2)
                    act.copy(mT[:], ps[:, 4, :]).then_inc(mT_ok, 1)

            def rows_in(b):
                act.wait_ge(gx_tr, b + 1)
                act.copy(xgT.rearrange("p c q -> p (c q)"), ps[:, 2, 0:D]).then_inc(gxT_ok, 1)

            def result(b, j, first):
                e = act.value_load(eb[0:1, ds(b, 1)], min_val=0, max_val=E - 1)
                act.wait_ge(o_mm, b + 1)
                if not first:
                    act.wait_ge(sc_out, (b - 2) * 16)
                act.activation(ob[:, j, :], ps[:, 4, 0:D], ACT.Copy, scale=xg[:, j, ds(e + D, 1)]).then_inc(ob_ok, 1)

            def step(i, first, last):
                for j in range(GR if not last else BLK - i * GR):
                    b = i * GR + j
                    act.wait_ge(h_mm, b + 1)
                    act.activation(sg, ps[:, 0, :], ACT.Silu).then_inc(sg_ok, 1)
                    if not (last and b == BLK - 1):
                        rows_in(b + 1)
                    if not (first and j == 0):
                        result(b - 1, (j - 1) % GR, first)

            act.wait_ge(eb_ok, 1)
            rows_in(0)
            step(0, True, False)
            with act.Fori(1, LAST) as i:
                step(i, False, False)
            step(LAST, False, True)
            result(BLK - 1, (BLK - 1) % GR, False)

        @block.vector
        def _(dve):
            dve.wait_ge(iotas, 12)
            dve.tensor_scalar(ident[:], iota_f[:], iota_p[:, 0:1], None, ALU.is_equal).then_inc(consts, 1)
            dve.tensor_scalar(tri[:], iota_f[:], iota_p[:, 0:1], None, ALU.is_gt).then_inc(consts, 1)
            dve.memset(ones[:], 1.0).then_inc(consts, 1)
            dve.tensor_scalar(sel_e[:], iota_p[:], float(ONE), None, ALU.is_equal).then_inc(consts, 1)
            dve.tensor_scalar(sel_o[:], iota_p[:], float(HS + ONE), None, ALU.is_equal).then_inc(consts, 1)
            dve.tensor_scalar(neg[:], iota_f[:, 0:H], iota_p[:, 0:1], -1.0, ALU.is_equal, ALU.mult).then_inc(consts, 1)
            dve.tensor_scalar(lt8[:], cum[:], 0.0, None, ALU.is_ge).then_inc(consts, 1)

            def stats(b):
                dve.wait_ge(x_in[b], 16)
                for t in range(b * TB, (b + 1) * TB):
                    dve.bn_stats(st[:, t, :], X[:, t, :]).then_inc(ln_st, 1)
                dve.wait_ge(ln_st, (b + 1) * TB)
                for t in range(b * TB, (b + 1) * TB):
                    dve.bn_aggr(mv[:, t, :], st[:, t, :]).then_inc(ln_mv, 1)
                dve.wait_ge(ln_mv, (b + 1) * TB)
                dve.tensor_scalar(rs[:, b * TB:(b + 1) * TB], mv[:, b * TB:(b + 1) * TB, 1], EPS, None, ALU.add
                                  ).then_inc(ln_v, 1)

            stats(0)
            dve.memset(ks, 0.0).then_inc(consts, 1)
            dve.memset(qs[:], 0.0).then_inc(consts, 1)
            dve.memset(mx[:], 0.0).then_inc(consts, 1)
            dve.memset(vc[:], 0.0).then_inc(consts, 1)
            dve.wait_ge(consts, 11)
            dve.memset(qs[:, :, ONE:ONE + 1], 1.0).then_inc(consts, 1)
            dve.wait_ge(kv_mm, 1)
            kv = ps[0:NK, 1, 0:B * 2 * DH].rearrange("p (b n) -> p b n", b=B)
            for b in range(B):
                for o in range(2):
                    for at in (HI_A, LO_A):
                        dve.tensor_scalar(ks[:, b, o, o * HS + at:o * HS + at + DH].bitcast(F32R),
                                          kv[:, b, 0:DH], SCALE, None, ALU.mult).then_inc(ks_hi, 1)
            dve.tensor_copy(mvb[:], kv[:, :, DH:2 * DH]).then_inc(ks_ok, 1)
            dve.wait_ge(ks_hi, 4 * B)
            for b in range(B):
                for o in range(2):
                    dve.scalar_tensor_tensor(ks[:, b, o, o * HS + HI_B:o * HS + HI_B + DH], kv[:, b, 0:DH], SCALE,
                                             ks[:, b, o, o * HS:o * HS + DH], ALU.mult, ALU.subtract
                                             ).then_inc(ks_ok, 1)
            dve.wait_ge(bd0_ok, 1)
            dve.wait_ge(consts, 12)

            def score_rows(b, j):
                if j >= 2:
                    dve.wait_ge(x_tr, b * HT + j - 1)
                for t in range(2 * j, 2 * j + 2):
                    q = b * TB + t
                    dve.tensor_scalar(xn[:, t % HT, :], X[:, q, :], mv[:, q, 0:1], rs[:, q:q + 1],
                                      ALU.subtract, ALU.mult).then_inc(xn_ok, 1)

            def scores(b, j):
                n = b * HT + j
                dve.wait_ge(q_sc, n + 1)
                dve.tensor_copy(sc[:, 2 * n:2 * n + 2, :], ps[:, 2, 0:2 * NK].rearrange("p (t n) -> p t n", n=NK)
                                ).then_inc(sc_ok, 1)

            def picks(b):
                here = slice(b * TB, (b + 1) * TB)
                dve.wait_ge(sc_ok, (b + 1) * HT)
                dve.tensor_reduce(m1[:, here], sc[:, here], AX.X, ALU.max).then_inc(am, 1)
                dve.wait_ge(am, 4 * b + 1)
                dve.tensor_tensor(eqw[:, here], sc[:, here], m1[:, here].unsqueeze(2).broadcast_to([P, TB, NK]),
                                  ALU.is_equal).then_inc(am, 1)
                dve.wait_ge(am, 4 * b + 2)
                dve.tensor_tensor(eqw[:, here], eqw[:, here], desc[:].unsqueeze(1).broadcast_to([P, TB, NK]), ALU.mult
                                  ).then_inc(am, 1)
                dve.wait_ge(am, 4 * b + 3)
                dve.tensor_reduce(m2[:, here], eqw[:, here], AX.X, ALU.max).then_inc(am, 1)
                dve.wait_ge(am, 4 * b + 4)
                dve.tensor_tensor(oh[:, here], eqw[:, here], m2[:, here].unsqueeze(2).broadcast_to([P, TB, NK]),
                                  ALU.is_equal).then_inc(oh_ok, 1)

            def masks(b):
                dve.wait_ge(cnt_mm, b + 1)
                dve.tensor_scalar(bias[:, b, :], ps[:, 3, 0:NK], 0.5, MASK, ALU.is_lt, ALU.mult).then_inc(cnt_ok, 1)
                dve.tensor_copy(cc[:, b:b + 1], ps[0:NK, 3, NK:NK + 1]).then_inc(cnt_ok, 1)
                dve.wait_ge(cnt_ok, 2 * b + 2)
                for o, sel in enumerate((sel_e, sel_o)):
                    dve.scalar_tensor_tensor(bd[:, b, o * NK:(o + 1) * NK], bias[:, b, :], sel[:, 0:1],
                                             bd0[:, b, o * NK:(o + 1) * NK], ALU.mult, ALU.add).then_inc(bd_ok, 1)
                dve.tensor_scalar(vc[:, b, 0:DH], mvb[:, b, :], cc[:, b:b + 1], None, ALU.mult).then_inc(bd_ok, 1)
                dve.tensor_copy(vc[:, b, DH:DH + 1], cc[:, b:b + 1]).then_inc(bd_ok, 1)

            def normalise(w, p):
                for t in range(HT):
                    if XN_AT[t] == p:
                        q = w * HT + t
                        if q >= 2:
                            dve.wait_ge(px_tr, q - 1)
                        dve.tensor_scalar(xp[:, t % 2, :], X[:, q, :], mv[:, q, 0:1], rs[:, q:q + 1],
                                          ALU.subtract, ALU.mult).then_inc(xp_ok, 1)

            def prep_low(w, p):
                if p in P_AT:
                    q = w * HT + P_AT.index(p)
                    dve.wait_ge(q_hi, q + 1)
                    dve.tensor_tensor(qs[:, :, LO_A:LO_A + DH], ps[:, 4, 0:D].rearrange("p (h w) -> p h w", w=DH),
                                      qs[:, :, HI_A:HI_A + DH], ALU.subtract).then_inc(q_lo, 1)

            def maxima(w, z):
                t, g = divmod(z, 2)
                dve.wait_ge(l1_mm, w * 2 * HT + z + 1)
                if w and not z:
                    dve.wait_ge(mx_tr, w)
                dve.tensor_reduce(mx[:, t * H + g * 8:t * H + g * 8 + 8],
                                  ps[:, 6:8, 0:4 * NK].rearrange("p k (h n) -> p k h n", n=NK),
                                  AX.X, ALU.max).then_inc(mx_ok, 1)

            def post(v, k):
                here = slice(v * HT, (v + 1) * HT)
                if k in (2, 3):
                    g = k - 2
                    dve.wait_ge(wc_mm, 2 * v + g + 1)
                    xv = X[:, v * HT + 2 * g:v * HT + 2 * g + 2, :]
                    dve.tensor_tensor(xv, xv, ps[:, 3, :].rearrange("p (t d) -> p t d", d=D), ALU.add
                                      ).then_inc(x2_ok, 1)
                    dve.wait_ge(x2_ok, 2 * v + g + 1)
                    for i in range(2 * g, 2 * g + 2):
                        dve.bn_stats(st2[:, i, :], X[:, v * HT + i, :]).then_inc(st2_ok, 1)
                    for i in range(2 * g, 2 * g + 2):
                        dve.wait_ge(st2_ok, v * HT + i + 1)
                        dve.bn_aggr(mv2[:, i, :], st2[:, i, :]).then_inc(mv2_ok, 1)
                if k == 3:
                    dve.wait_ge(mv2_ok, v * HT + HT)
                    dve.tensor_scalar(rs2[:], mv2[:, :, 1], EPS, None, ALU.add).then_inc(v2_ok, 1)
                if k == 4:
                    dve.wait_ge(rs2_ok, v + 1)
                    dve.wait_ge(rows_out, 32 + 16 * v)
                    for i in range(HT):
                        dve.tensor_scalar(xn2[:, i, :], X[:, v * HT + i, :],
                                          mv2[:, i, 0:1], rs2[:, i:i + 1], ALU.subtract, ALU.mult).then_inc(xn2_ok, 1)
                if k not in (7, 8, 9):
                    return
                wide = lambda a: a.unsqueeze(2).broadcast_to([P, HT, E])
                dese = desc_e[:].unsqueeze(1).broadcast_to([P, HT, E])
                steps = 14
                done = [{7: 0, 8: 4, 9: 11}[k]]

                def link(ins):
                    done[0] += 1
                    ins.then_inc(top, 1)
                    dve.wait_ge(top, v * steps + done[0])

                if k == 7:
                    dve.wait_ge(r_mm, v + 1)
                    link(dve.tensor_copy(rl[:], ps[:, 3, 0:HT * E].rearrange("p (t e) -> p t e", e=E)))
                    link(dve.tensor_reduce(r1[:], rl[:], AX.X, ALU.max))
                    dve.tensor_tensor(lm[:], rl[:], wide(r1[:]), ALU.subtract).then_inc(lm_ok, 1)
                    link(dve.tensor_tensor(eq[:], rl[:], wide(r1[:]), ALU.is_equal))
                    link(dve.tensor_tensor(eq[:], eq[:], dese, ALU.mult))
                if k == 8:
                    link(dve.tensor_reduce(f1[:], eq[:], AX.X, ALU.max))
                    link(dve.tensor_tensor(o1[:, here, :], eq[:], wide(f1[:]), ALU.is_equal))
                    link(dve.scalar_tensor_tensor(rl[:], o1[:, here, :], -1e38, rl[:], ALU.mult, ALU.add))
                    link(dve.tensor_reduce(r1[:], rl[:], AX.X, ALU.max))
                    link(dve.tensor_tensor(eq[:], rl[:], wide(r1[:]), ALU.is_equal))
                    link(dve.tensor_tensor(eq[:], eq[:], dese, ALU.mult))
                    link(dve.tensor_reduce(f1[:], eq[:], AX.X, ALU.max))
                    dve.tensor_tensor(o2[:, here, :], eq[:], wide(f1[:]), ALU.is_equal).then_inc(rl_ok, 1)
                if k == 9:
                    dve.wait_ge(rl_ok, v + 1)
                    dve.tensor_tensor(cnt[:, here, :], o1[:, here, :], o2[:, here, :], ALU.add).then_inc(cnt_s, 1)
                    dve.wait_ge(exr_ok, v + 1)
                    link(dve.tensor_reduce(sme[:], ex[:], AX.X, ALU.add))
                    link(dve.reciprocal(sme[:], sme[:]))
                    dve.wait_ge(cnt_s, v + 1)
                    link(dve.tensor_tensor(ex[:], ex[:], cnt[:, here, :], ALU.mult))
                    dve.tensor_tensor(xr[:, :, D:RW], ex[:], wide(sme[:]), ALU.mult).then_inc(rows_ok, 1)

            def sums(u, p):
                if p % 2 == 0 and p >= 2:
                    n = u * NG + p // 2 - 1
                    dve.wait_ge(pv_mm, n + 1)
                    if n >= 2:
                        dve.wait_ge(tu_mm, n - 1)
                    dve.tensor_copy(uT[:, n % 2, :], ps[:, 2, :]).then_inc(ut_ok, 1)
                if p % 2 == 1 and p >= 3:
                    g = (p - 3) // 2
                    n = u * NG + g
                    dve.wait_ge(tu_mm, n + 1)
                    if u and g == 0:
                        dve.wait_ge(o_tr, 2 * u)
                    uv = ps[:, 2, :].rearrange("p (t h w) -> p t h w", h=4, w=UH)
                    dve.reciprocal(rden[:], uv[:, :, :, DH]).then_inc(rd_ok, 1)
                    dve.wait_ge(rd_ok, n + 1)
                    dve.tensor_tensor(on[:].rearrange("p t (h w) -> p t h w", w=DH)[:, :, 4 * g:4 * g + 4, :],
                                      uv[:, :, :, 0:DH], rden[:].unsqueeze(3).broadcast_to([P, HT, 4, DH]), ALU.mult
                                      ).then_inc(on_ok, 1)

            dve.wait_ge(ln_r, 1)
            score_rows(0, 0)
            score_rows(0, 1)
            for j in range(HT):
                scores(0, j)
                if j + 2 < HT:
                    score_rows(0, j + 2)
            picks(0)
            for u in range(-1, NH + 1):
                for p in range(SLOTS):
                    if u < 0:
                        if p == 0:
                            normalise(0, 0)
                            stats(1)
                            dve.memset(xr[:], 0.0).then_inc(pad_ok, 1)
                        if p == MASKS_AT[0]:
                            masks(0)
                            dve.wait_ge(ln_r, B)
                        if p in SCORES_AT:
                            score_rows(1, SCORES_AT.index(p))
                        if p - 1 in SCORES_AT:
                            scores(1, SCORES_AT.index(p - 1))
                    elif p == 0 and u + 1 < NH:
                        normalise(u + 1, p)
                    if u + 1 < NH and 2 <= p <= 2 * HT + 1:
                        maxima(u + 1, p - 2)
                    if u >= 1 and p == 0:
                        sums(u - 1, SLOTS - 1)
                    if 0 <= u < NH and p:
                        sums(u, p - 1)
                    if u + 1 < NH:
                        prep_low(u + 1, p)
                        if p:
                            normalise(u + 1, p)
                    if u < 0 and p == PICKS_AT:
                        picks(1)
                    if u < 0 and p == MASKS_AT[1]:
                        masks(1)
                    if u >= 2 and p == 0:
                        post(u - 2, SLOTS - 1)
                    if u >= 1 and p:
                        post(u - 1, p - 1)
            post(NH - 1, SLOTS - 1)

            links = [0]

            def link(ins):
                links[0] += 1
                ins.then_inc(rt, 1)
                dve.wait_ge(rt, links[0])

            dve.wait_ge(pre_mm, 1)
            link(dve.tensor_tensor(ce[:], ps[:, 1, 0:E].unsqueeze(2).broadcast_to([P, E, T]),
                                   k128[:].unsqueeze(1).broadcast_to([P, E, T]), ALU.is_gt))
            link(dve.tensor_reduce(nb[:], ce[:], AX.X, ALU.add))
            link(dve.tensor_tensor(cum[:], lt8[:], nb[:].unsqueeze(1).broadcast_to([P, E, E]), ALU.mult))
            link(dve.tensor_reduce(end[:], cum[:], AX.X, ALU.add))
            link(dve.tensor_tensor(base[:], end[:], nb[:], ALU.subtract))
            link(dve.tensor_scalar(base[:], base[:], float(P), None, ALU.mult))
            link(dve.tensor_tensor(slf[:], ps[:, 0, 0:T * E].rearrange("p (t e) -> p t e", e=E),
                                   base[:].unsqueeze(1).broadcast_to([P, T, E]), ALU.add))
            for k, o in enumerate((o1, o2)):
                link(dve.tensor_tensor(pick[:], slf[:], o[:], ALU.mult))
                link(dve.tensor_reduce(slot[:, k, :], pick[:], AX.X, ALU.add))
            link(dve.tensor_copy(sloti[:], slot[:].rearrange("p k t -> p (k t)")))
            link(dve.tensor_scalar(bki[:], sloti[:], 7, None, ALU.logical_shift_right))
            link(dve.tensor_scalar(rmi[:], sloti[:], P - 1, None, ALU.bitwise_and))
            link(dve.tensor_copy(bkh[:], bki[:]))
            link(dve.tensor_copy(rmh[:], rmi[:]))
            link(dve.tensor_tensor(bsel, blk_h[:].unsqueeze(1).broadcast_to([P, 2 * T, BLK]),
                                   bkh[:].unsqueeze(2).broadcast_to([P, 2 * T, BLK]), ALU.is_equal))
            for k in range(2):
                link(dve.tensor_tensor(bval[:, k * T:(k + 1) * T, :], bsel[:, k * T:(k + 1) * T, :],
                                       tok_h[:].unsqueeze(2).broadcast_to([P, T, BLK]), ALU.mult))

            for n in range(0, 2 * T, 8):
                dve.tensor_tensor(asel[:, n:n + 8, :], iota_h[:].unsqueeze(1).broadcast_to([P, 8, P]),
                                  rmh[:, n:n + 8].unsqueeze(2).broadcast_to([P, 8, P]), ALU.is_equal
                                  ).then_inc(asel_ok, 1)
            dve.wait_ge(asel_used, 1)
            link(dve.tensor_copy(tokp[:], ps[:, 2, 0:BLK]))
            link(dve.tensor_scalar(idf[:], tokp[:], 0.0, spare[:, 0:1], ALU.is_equal, ALU.mult))
            dve.scalar_tensor_tensor(idx[:], tokp[:], -1.0, idf[:], ALU.add, ALU.add).then_inc(idx_ok, 1)
            link(dve.tensor_tensor(ebc, blk_f[:].unsqueeze(2).broadcast_to([P, BLK, E]),
                                   end[:].unsqueeze(1).broadcast_to([P, BLK, E]), ALU.is_ge))
            link(dve.tensor_reduce(ebf[:], ebc, AX.X, ALU.add))
            dve.tensor_scalar(eb[:], ebf[:], float(E - 1), None, ALU.min).then_inc(eb_ok, 1)

            def step(i, blocks):
                for j in range(blocks):
                    b = i * GR + j
                    dve.wait_ge(sg_ok, b + 1)
                    dve.tensor_tensor(yb, sg, ps[:, 1, :], ALU.mult).then_inc(y_ok, 1)
                    dve.wait_ge(y_tr, b + 1)
                    dve.tensor_copy(yT[:].rearrange("p c q -> p (c q)"), ps[:, 3, :]).then_inc(yT_ok, 1)

            with dve.Fori(0, LAST) as i:
                step(i, GR)
            step(LAST, BLK - LAST * GR)

        @block.tensor
        def _(pe):
            pe.wait_ge(wts_in, 16 * 6)
            for c in range(DC):
                for k in range(DC):
                    mm = pe.matmul(ps[:, 0, c * B * NK:(c + 1) * B * NK], WQ[:, k, c * P:(c + 1) * P], CT[:, k, :],
                                   start=(k == 0), stop=(k == DC - 1))
            mm.then_inc(g_mm, 1)
            for b in range(B):
                for k in range(DC):
                    mm = pe.matmul(ps[0:NK, 1, b * 2 * DH:(b + 1) * 2 * DH], CT[:, k, b * NK:(b + 1) * NK], WKV[:, k, :],
                                   start=(k == 0), stop=(k == DC - 1))
            mm.then_inc(kv_mm, 1)
            pe.wait_ge(consts, 12)
            pe.wait_ge(ks_ok, 2 * B + 1)
            for n in range(2 * B):
                mm = pe.transpose(ps[:, 2, n * P:n * P + NK], ks[:, n // 2, n % 2, :], ident[0:NK, 0:NK])
            mm.then_inc(ks_tr, 1)
            pe.wait_ge(g_out, 1)
            pe.wait_ge(bd0_ok, 1)

            def score_turn(b, j):
                pe.wait_ge(xn_ok, b * TB + 2 * j + 2)
                if b or j >= 2:
                    pe.wait_ge(xT_ok, b * HT + j - 1)
                for t in range(2):
                    for c in range(DC):
                        mm = pe.transpose(ps[:, j % 2, (t * DC + c) * P:(t * DC + c + 1) * P],
                                          xn[:, 2 * (j % 2) + t, c * P:(c + 1) * P], ident[:])
                mm.then_inc(x_tr, 1)

            def score(b, j):
                n = b * HT + j
                pe.wait_ge(xT_ok, n + 1)
                if n:
                    pe.wait_ge(sc_ok, n)
                for t in range(2):
                    for c in range(DC):
                        mm = pe.matmul(ps[:, 2, t * NK:(t + 1) * NK], xT[:, 2 * (j % 2) + t, c, :], GT[:, c, b, :],
                                       start=(c == 0), stop=(c == DC - 1))
                mm.then_inc(q_sc, 1)

            def counts(b):
                pe.wait_ge(oh_ok, b + 1)
                if b:
                    pe.wait_ge(cnt_ok, 2 * b)
                for t in range(b * TB, (b + 1) * TB):
                    pe.matmul(ps[:, 3, 0:NK], ones[:], oh[:, t, :], start=(t % TB == 0), stop=(t % TB == TB - 1))
                for t in range(b * TB, (b + 1) * TB):
                    mm = pe.matmul(ps[0:NK, 3, NK:NK + 1], oh[:, t, :], ones[:, 0:1],
                                   start=(t % TB == 0), stop=(t % TB == TB - 1))
                mm.then_inc(cnt_mm, 1)

            def prep_x(w, t):
                q = w * HT + t
                pe.wait_ge(xp_ok, q + 1)
                if q:
                    pe.wait_ge(q_lo, q)
                if w and t == 0:
                    pe.wait_ge(mT_ok, w)
                for c in range(DC):
                    mm = pe.transpose(ps[:, 4, c * P:(c + 1) * P], xp[:, t % 2, c * P:(c + 1) * P], ident[:])
                mm.then_inc(px_tr, 1)

            def prep_project(w, t):
                q = w * HT + t
                pe.wait_ge(pxT_ok, q + 1)
                for c in range(DC):
                    mm = pe.matmul(ps[:, 4, 0:D], xpT[:, t % 2, c, :], WQT[:, c, :], start=(c == 0), stop=(c == DC - 1))
                mm.then_inc(q_mm, 1)

            def prep_turn(w, z):
                t, g = divmod(z, 2)
                pe.wait_ge(q_lo, w * HT + t + 1)
                if w or z:
                    pe.wait_ge(qT_ok, w * 2 * HT + z)
                for n in range(4):
                    a = 2 * (4 * g + n)
                    mm = pe.transpose(ps[:, 5, n * P:(n + 1) * P], qs[:, a:a + 2, :].rearrange("p h w -> p (h w)"),
                                      ident[:])
                mm.then_inc(q_tr, 1)

            def prep_logits(w, z):
                t, g = divmod(z, 2)
                if w % 2 == 0 and z == 0:
                    pe.wait_ge(bd_ok, 4 * (w // 2 + 1))
                pe.wait_ge(qT_ok, w * 2 * HT + z + 1)
                if w or z:
                    pe.wait_ge(mx_ok, w * 2 * HT + z)
                for n in range(4):
                    mm = pe.matmul(ps[:, 6 + n // 2, (n % 2) * 2 * NK:(n % 2 + 1) * 2 * NK],
                                   qT[:, w % 2, 4 * g + n, t * P:(t + 1) * P], bd[:, w // 2, :], start=True, stop=True)
                mm.then_inc(l1_mm, 1)

            def prep_maxima(w):
                pe.wait_ge(mx_ok, (w + 1) * 2 * HT)
                for i in range(HT):
                    mm = pe.transpose(ps[:, 4, i * P:(i + 1) * P], mx[:, i * H:i * H + P], ident[:])
                mm.then_inc(mx_tr, 1)

            def logits(u, p):
                n = u * NP + p
                if p == 0:
                    pe.wait_ge(mT_ok, u + 1)
                if n:
                    pe.wait_ge(ex_ok, n)
                for o in range(2):
                    pe.matmul(ps[0:NK, o, :], bd[:, u // 2, o * NK:(o + 1) * NK], qT[:, u % 2, p, :],
                              start=True, stop=False)
                    mm = pe.matmul(ps[0:NK, o, :], neg[:, 2 * p + o:2 * p + o + 1].broadcast_to([P, NK]), mT[:],
                                   start=False, stop=True)
                mm.then_inc(l2_mm, 1)

            def sums(u, p):
                if p % 2 == 0 and p >= 2:
                    g = p // 2 - 1
                    n = u * NG + g
                    pe.wait_ge(ex_ok, u * NP + 2 * g + 2)
                    if n:
                        pe.wait_ge(on_ok, n)
                    for h in range(4):
                        mm = pe.matmul(ps[h * UH:(h + 1) * UH, 2, :], vc[:, u // 2, :], pT[0:NK, 4 * (n % 2) + h, :],
                                       start=True, stop=True)
                    mm.then_inc(pv_mm, 1)
                if p % 2 == 1 and p >= 3:
                    n = u * NG + (p - 3) // 2
                    pe.wait_ge(ut_ok, n + 1)
                    for i in range(HT):
                        mm = pe.transpose(ps[:, 2, i * P:(i + 1) * P], uT[:, n % 2, i * P:(i + 1) * P], ident[:])
                    mm.then_inc(tu_mm, 1)

            def turn(src, g, done):
                for i in range(2 * g, 2 * g + 2):
                    for c in range(DC):
                        mm = pe.transpose(ps[:, 3, ((i % 2) * DC + c) * P:((i % 2) * DC + c + 1) * P],
                                          src[:, i, c * P:(c + 1) * P], ident[:])
                mm.then_inc(done, 1)

            def post(v, k):
                if k == 0:
                    pe.wait_ge(on_ok, (v + 1) * NG)
                    turn(on, 0, o_tr)
                if k == 1:
                    pe.wait_ge(oT_ok, 2 * v + 1)
                    turn(on, 1, o_tr)
                if k in (2, 3):
                    g = k - 2
                    pe.wait_ge(oT_ok, 2 * v + 2)
                    if g:
                        pe.wait_ge(x2_ok, 2 * v + 1)
                    for i in range(2 * g, 2 * g + 2):
                        for c in range(DC):
                            mm = pe.matmul(ps[:, 3, (i % 2) * D:(i % 2 + 1) * D], oT[:, i, c, :], WC[:, c, :],
                                           start=(c == 0), stop=(c == DC - 1))
                    mm.then_inc(wc_mm, 1)
                if k == 5:
                    pe.wait_ge(xn2_ok, (v + 1) * HT)
                    turn(xn2, 0, x2_tr)
                if k == 6:
                    pe.wait_ge(x2T_ok, 2 * v + 1)
                    turn(xn2, 1, x2_tr)
                if k == 7:
                    pe.wait_ge(x2T_ok, 2 * v + 2)
                    for i in range(HT):
                        for c in range(DC):
                            mm = pe.matmul(ps[:, 3, i * E:(i + 1) * E], oT[:, i, c, :], RT[:, c, :],
                                           start=(c == 0), stop=(c == DC - 1))
                    mm.then_inc(r_mm, 1)

            score_turn(0, 0)
            for j in range(HT):
                if j + 1 < HT:
                    score_turn(0, j + 1)
                score(0, j)
            for u in range(-1, NH + 1):
                prepares = u + 1 < NH
                for p in range(SLOTS):
                    if prepares and 1 <= p <= 2 * HT:
                        prep_turn(u + 1, p - 1)
                    if u < 0 and p in MASKS_AT:
                        counts(MASKS_AT.index(p))
                    if 0 <= u < NH and 1 <= p <= NP:
                        logits(u, p - 1)
                    if prepares and 2 <= p <= 2 * HT + 1:
                        prep_logits(u + 1, p - 2)
                    if u >= 1 and p == 0:
                        sums(u - 1, SLOTS - 1)
                    if 0 <= u < NH and p:
                        sums(u, p - 1)
                    if prepares and p in X_AT:
                        prep_x(u + 1, X_AT.index(p))
                    if prepares and p in P_AT:
                        prep_project(u + 1, P_AT.index(p))
                    if u < 0 and p in SCORES_AT:
                        score_turn(1, SCORES_AT.index(p))
                        score(1, SCORES_AT.index(p))
                    if u >= 1 and p:
                        post(u - 1, p - 1)
                if prepares:
                    prep_maxima(u + 1)

            pe.wait_ge(cnt_s, NH)
            pe.matmul(ps[:, 0, 0:T * E], tri[:], cnt[:].rearrange("p t e -> p (t e)"), start=True, stop=False)
            for t in range(T - 1):
                pe.matmul(ps[:, 0, (t + 1) * E:T * E].rearrange("p (t e) -> p t e", e=E), ones[:],
                          cnt[:, t, :].unsqueeze(1).broadcast_to([P, T - 1 - t, E]), start=False, stop=(t == T - 2))
            for t in range(T):
                mm = pe.matmul(ps[:, 1, 0:E], ones[:], cnt[:, t, :], start=(t == 0), stop=(t == T - 1))
            mm.then_inc(pre_mm, 1)
            for n in range(2 * T):
                if n % 8 == 0:
                    pe.wait_ge(asel_ok, n // 8 + 1)
                mm = pe.matmul(ps[:, 2, 0:BLK], asel[:, n, :], bval[:, n, :], start=(n == 0), stop=(n == 2 * T - 1))
            mm.then_inc(asel_used, 1)

            pe.wait_ge(expw_in, 16 * 2 * E)
            pe.wait_ge(eb_ok, 1)
            pe.wait_ge(idx_ok, 1)

            def turn_rows(j, value):
                pe.wait_ge(g_in[j], value)
                for c in range(DC):
                    mm = pe.transpose(ps[:, 2, c * P:(c + 1) * P], xg[:, j, c * P:(c + 1) * P], ident[:])
                mm.then_inc(gx_tr, 1)

            def inner(b, e):
                pe.wait_ge(gxT_ok, b + 1)
                for f in range(2):
                    for c in range(DC):
                        mm = pe.matmul(ps[:, f, :], xgT[:, c, :],
                                       W1[:, ds(e, 1), c, f * FI:(f + 1) * FI].rearrange("p a n -> p (a n)"),
                                       start=(c == 0), stop=(c == DC - 1))
                mm.then_inc(h_mm, 1)

            def outer(b, e):
                pe.wait_ge(yT_ok, b + 1)
                for c in range(FC):
                    mm = pe.matmul(ps[:, 4, 0:D], yT[:, c, :], W2[:, ds(e, 1), c, :].rearrange("p a n -> p (a n)"),
                                   start=(c == 0), stop=(c == FC - 1))
                mm.then_inc(o_mm, 1)

            def turn_y(b):
                pe.wait_ge(y_ok, b + 1)
                for c in range(FC):
                    mm = pe.transpose(ps[:, 3, c * P:(c + 1) * P], yb[:, c * P:(c + 1) * P], ident[:])
                mm.then_inc(y_tr, 1)

            def expert(b):
                return pe.value_load(eb[0:1, ds(b, 1)], min_val=0, max_val=E - 1)

            def step(i, first, last):
                e_last = expert(i * GR - 1) if not first else None
                e = expert(i * GR)
                blocks = BLK - i * GR if last else GR
                for j in range(blocks):
                    b = i * GR + j
                    inner(b, e)
                    e_next = expert(b + 1) if j < blocks - 1 else None
                    if not (last and j == blocks - 1):
                        turn_rows((j + 1) % GR, i * 16 + (16 if j < GR - 1 else 32))
                    if not (first and j == 0):
                        if not (first and j == 1):
                            pe.wait_ge(ob_ok, b - 1)
                        outer(b - 1, e_last)
                    turn_y(b)
                    e_last, e = e, e_next
                return e_last

            turn_rows(0, 16)
            step(0, True, False)
            with pe.Fori(1, LAST) as i:
                step(i, False, False)
            e = step(LAST, False, True)
            pe.wait_ge(ob_ok, BLK - 1)
            outer(BLK - 1, e)


def kernel(x, ctx_1024, L0_xattn_Wq, L0_xattn_Wkv, L0_xattn_Wc, L0_ffn_w1, L0_ffn_w2, L0_ffn_router_w):
    import numpy as np
    from concourse import bacc
    from concourse.bass_utils import run_bass_kernel_spmd

    nc = bacc.Bacc("TRN2", target_bir_lowering=False, num_devices=1)
    laid = {
        "x": np.asarray(x).reshape(B * S, D),
        "ctxT": np.asarray(ctx_1024).reshape(B * NK, D).T,
        "Wq": np.asarray(L0_xattn_Wq),
        "WqT": np.asarray(L0_xattn_Wq).T,
        "WkvT": np.asarray(L0_xattn_Wkv).T,
        "WcT": np.asarray(L0_xattn_Wc).T,
        "routerT": np.asarray(L0_ffn_router_w).T,
        "w1T": np.asarray(L0_ffn_w1).transpose(0, 2, 1),
        "w2T": np.asarray(L0_ffn_w2).transpose(0, 2, 1),
    }
    arrays, args = {}, {}
    for name, a in laid.items():
        arrays[f"in_{name}"] = np.ascontiguousarray(a)
        args[name] = nc.dram_tensor(f"in_{name}", a.shape, mybir.dt.from_np(a.dtype), kind="ExternalInput").ap()
    args["out"] = nc.dram_tensor("out_x", [B * S + P, D], F32, kind="ExternalOutput").ap()
    build(nc, **args)
    r = run_bass_kernel_spmd(nc, [arrays], core_ids=[0])
    return r.results[0]["out_x"][0:B * S].reshape(B, S, D)
```

```python
from contextlib import ExitStack

import concourse.bass as bass
from concourse import mybir

F32 = mybir.dt.float32
F32R = mybir.dt.float32r
F16 = mybir.dt.float16
BF16 = mybir.dt.bfloat16
I32 = mybir.dt.int32
U32 = mybir.dt.uint32
ALU = mybir.AluOpType
ACT = mybir.ActivationFunctionType
AX = mybir.AxisListType
ds = bass.ds

P = 128
D = 256
DC = D // P
B = 2
S = 1024
TB = S // P
T = B * TB
HT = TB // 2
NH = T // HT
NK = 77
H = 16
DH = D // H
NP = H // 2
HS = P // 2
UH = 32
NG = H // 4
RW = D + 8
E = 8
FI = 512
FC = FI // P
BLK = 2 * S * B // P + E - 1
GR = 4
LAST = (BLK - 1) // GR
CW = 512
WC1 = DC * 2 * FI // CW
WC2 = FC * D // CW
EC = WC1 + WC2
NC = E * EC
SCALE = 0.25
MASK = -1e30
EPS = 1e-5
assert HT >= GR and DH ** -0.5 == SCALE

SLOTS = NP + 2
XN_AT = (-3, -1, 1, 3)
X_AT = (-2, 0, 2, 4)
P_AT = (-1, 1, 3, 5)
SCORES_AT = (1, 2, 3, 4)
PICKS_AT = 5
MASKS_AT = (1, 8)
P2_AT = 4

HI_A, LO_A, ONE, HI_B = 0, DH, 2 * DH, 3 * DH


def due(at, u, p):
    for w in range(NH):
        for t in range(HT):
            if w * SLOTS + at[t] == (u + 1) * SLOTS + p:
                return w, t
    return None


def build(nc, x, ctxT, Wq, WqT, WkvT, WcT, routerT, w, out):
    rows = nc.dram_tensor("rows", [(T + 1) * P, RW], F32).ap()
    lows = nc.dram_tensor("lows", [NC, P, CW], BF16).ap()
    with ExitStack() as ctx:
        def sb(name, shape, dt=F32):
            return ctx.enter_context(nc.sbuf_tensor(name, shape, dt))

        def sem(name):
            return ctx.enter_context(nc.semaphore(name))

        ps = ctx.enter_context(nc.psum_tensor("ps", [P, 8, 512], F32))

        iota_f = sb("iota_f", [P, P])
        iota_p = sb("iota_p", [P, 1])
        iota_h = sb("iota_h", [P, P], F16)
        blk_h = sb("blk_h", [P, BLK], F16)
        blk_f = sb("blk_f", [P, BLK])
        tok_h = sb("tok_h", [P, T], F16)
        spare = sb("spare", [P, 1])
        k128 = sb("k128", [P, T])
        desc = sb("desc", [P, NK], BF16)
        desc_e = sb("desc_e", [P, E])
        lt8 = sb("lt8", [P, E, E])
        ident = sb("ident", [P, P])
        tri = sb("tri", [P, P], BF16)
        ones = sb("ones", [P, P], BF16)
        sel_e = sb("sel_e", [P, 1])
        sel_o = sb("sel_o", [P, 1])
        neg = sb("neg", [P, H], F32R)
        half = sb("half", [P, T])
        X = sb("X", [P, T, D])
        WQT = sb("WQT", [P, DC, D])
        GT = sb("GT", [P, DC, B, NK])
        WKV = sb("WKV", [P, DC, 2 * DH])
        WC = sb("WC", [P, DC, D])
        RT = sb("RT", [P, DC, E])
        mvb = sb("mvb", [NK, B, DH])
        bd = sb("bd", [P, B, 2 * NK], F32R)
        vc = sb("vc", [NK, B, UH])
        cc = sb("cc", [NK, B])
        st = sb("st", [P, T, 6])
        mv = sb("mv", [P, T, 2])
        rs = sb("rs", [P, T])
        xp = sb("xp", [P, 2, D])
        xpT = sb("xpT", [P, 2, DC, P])
        qs = sb("qs", [P, H, HS])
        m1 = sb("m1", [P, T])
        m2 = sb("m2", [P, T])
        mx = sb("mx", [P, (HT - 1) * H + P])
        mT = sb("mT", [P, HT * P], F32R)
        pT = sb("pT", [P, 8, 512])
        uT = sb("uT", [P, 2, 512])
        rden = sb("rden", [P, HT, 4])
        on = sb("on", [P, HT, D])
        oT = sb("oT", [P, HT, DC, P])
        st2 = sb("st2", [P, HT, 6])
        mv2 = sb("mv2", [P, HT, 2])
        rs2 = sb("rs2", [P, HT])
        xr = sb("xr", [P, HT, RW])
        xn2 = xr[:, :, 0:D]
        rl = sb("rl", [P, HT, E])
        r1 = sb("r1", [P, HT])
        f1 = sb("f1", [P, HT])
        eq = sb("eq", [P, HT, E])
        lm = sb("lm", [P, HT, E])
        ex = sb("ex", [P, HT, E])
        sme = sb("sme", [P, HT])
        o1 = sb("o1", [P, T, E])
        o2 = sb("o2", [P, T, E])
        cnt = sb("cnt", [P, T, E], BF16)
        nb = sb("nb", [P, E])
        cum = sb("cum", [P, E, E])
        end = sb("end", [P, E])
        base = sb("base", [P, E])
        slot = sb("slot", [P, 2, T])
        sloti = sb("sloti", [P, 2 * T], I32)
        bki = sb("bki", [P, 2 * T], I32)
        rmi = sb("rmi", [P, 2 * T], I32)
        bkh = sb("bkh", [P, 2 * T], F16)
        rmh = sb("rmh", [P, 2 * T], F16)
        ebf = sb("ebf", [P, BLK])
        eb = sb("eb", [P, BLK], I32)
        tokp = sb("tokp", [P, BLK])
        idf = sb("idf", [P, BLK])
        idx = sb("idx", [P, BLK], U32)
        low = sb("low", [P, 2, CW], BF16)
        with nc.sbuf_tensor("raw", [P, NC + 2, CW], F32) as raw:
            pass
        W = sb("W", [P, NC + 2, CW], F32R)
        with nc.sbuf_tensor("qT", [P, 2, NP, HT * P], F32R) as qT:
            pass
        W1lo = sb("W1lo", [P, E * WC1, CW], BF16)
        pT1 = pT[:].rearrange("p n q -> p (n q)")
        ns = T * NK
        sc = pT1[:, 0:ns].rearrange("p (t n) -> p t n", n=NK)
        eqw = pT1[:, ns:3 * ns // 2].bitcast(BF16).rearrange("p (t n) -> p t n", n=NK)
        oh = pT1[:, 3 * ns // 2:2 * ns].bitcast(BF16).rearrange("p (t n) -> p t n", n=NK)
        bias = pT1[:, 2 * ns + 2 * B * NK:2 * ns + 3 * B * NK].rearrange("p (b n) -> p b n", b=B)
        bd0 = pT1[:, 2 * ns:2 * ns + 2 * B * NK].rearrange("p (b n) -> p b n", b=B)
        nh = 2 * T * BLK // 2
        bsel = pT1[:, 0:nh].bitcast(F16).rearrange("p (t b) -> p t b", b=BLK)
        bval = pT1[:, nh:2 * nh].bitcast(F16).rearrange("p (t b) -> p t b", b=BLK)
        ebc = pT1[:, 2 * nh:2 * nh + BLK * E].rearrange("p (b e) -> p b e", e=E)
        asel = pT1[:, 2 * nh + BLK * E:2 * nh + BLK * E + T * P].bitcast(F16).rearrange("p (n q) -> p n q", q=P)
        at = 2 * nh + BLK * E + T * P
        slf, pick = (pT1[:, at + k * T * E:at + (k + 1) * T * E].rearrange("p (t e) -> p t e", e=E) for k in range(2))
        ce = pT1[:, at + 2 * T * E:at + 3 * T * E].rearrange("p (e t) -> p e t", t=T)
        xn = on
        xT = oT
        ks = oT[0:NK, 2:4].rearrange("p t c q -> p (t c q)").rearrange("p (b o n) -> p b o n", b=B, o=2)
        qs1 = qs[:].rearrange("p h w -> p (h w)")
        xg = xr
        x_hi = qs1[:, 0:D].bitcast(F32R)
        x_lo = qs1[:, D:2 * D].bitcast(F32R)
        y_hi = mT
        y_lo = qs1[:, 2 * D:2 * D + FI].bitcast(F32R)
        xpT1 = xpT[:].rearrange("p a c q -> p (a c q)").bitcast(BF16)
        x_b = xpT1[:, 0:D]
        y_b = xpT1[:, D:D + FI]
        W2lo = X[:].rearrange("p t d -> p (t d)").bitcast(BF16).rearrange("p (n w) -> p n w", w=CW)
        sg = uT[:, 0, :]
        yb = uT[:, 1, :]
        ob = oT[:].rearrange("p t c q -> p t (c q)")
        uT1 = uT[:].rearrange("p a b -> p (a b)")
        WQ = uT1[:, 0:DC * D].rearrange("p (c n) -> p c n", c=DC)
        CT = uT1[:, DC * D:DC * (D + B * NK)].rearrange("p (c n) -> p c n", c=DC)

        x_in = [sem(f"x_in{i}") for i in range(B)]
        wts_in = sem("wts_in")
        raw_in = [sem(f"raw_in{e}") for e in range(E)]
        hi_ok = sem("hi_ok")
        low_ok = sem("low_ok")
        low_out = [sem(f"low_out{i}") for i in range(2)]
        low_in = sem("low_in")
        iotas = sem("iotas")
        consts = sem("consts")
        ln_st = sem("ln_st")
        ln_mv = sem("ln_mv")
        ln_v = sem("ln_v")
        ln_r = sem("ln_r")
        g_mm = sem("g_mm")
        g_out = sem("g_out")
        kv_mm = sem("kv_mm")
        ks_hi = sem("ks_hi")
        ks_ok = sem("ks_ok")
        ks_tr = sem("ks_tr")
        bd0_ok = sem("bd0_ok")
        xn_ok = sem("xn_ok")
        xp_ok = sem("xp_ok")
        x_tr = sem("x_tr")
        xT_ok = sem("xT_ok")
        px_tr = sem("px_tr")
        pxT_ok = sem("pxT_ok")
        q_mm = sem("q_mm")
        q_sc = sem("q_sc")
        q_hi = sem("q_hi")
        q_lo = sem("q_lo")
        sc_ok = sem("sc_ok")
        q_tr = sem("q_tr")
        qT_ok = sem("qT_ok")
        am = sem("am")
        oh_ok = sem("oh_ok")
        cnt_mm = sem("cnt_mm")
        cnt_ok = sem("cnt_ok")
        bd_ok = sem("bd_ok")
        l1_mm = sem("l1_mm")
        mx_ok = sem("mx_ok")
        mx_tr = sem("mx_tr")
        mT_ok = sem("mT_ok")
        l2_mm = sem("l2_mm")
        ex_ok = sem("ex_ok")
        pv_mm = sem("pv_mm")
        ut_ok = sem("ut_ok")
        tu_mm = sem("tu_mm")
        rd_ok = sem("rd_ok")
        on_ok = sem("on_ok")
        o_tr = sem("o_tr")
        oT_ok = sem("oT_ok")
        wc_mm = sem("wc_mm")
        x2_ok = sem("x2_ok")
        st2_ok = sem("st2_ok")
        mv2_ok = sem("mv2_ok")
        v2_ok = sem("v2_ok")
        rs2_ok = sem("rs2_ok")
        xn2_ok = sem("xn2_ok")
        rows_ok = sem("rows_ok")
        rows_out = sem("rows_out")
        x2_out = sem("x2_out")
        x2_tr = sem("x2_tr")
        x2T_ok = sem("x2T_ok")
        r_mm = sem("r_mm")
        top = sem("top")
        cnt_s = sem("cnt_s")
        rl_ok = sem("rl_ok")
        rt = sem("rt")
        lm_ok = sem("lm_ok")
        exr_ok = sem("exr_ok")
        pad_ok = sem("pad_ok")
        pre_mm = sem("pre_mm")
        asel_ok = sem("asel_ok")
        asel_used = sem("asel_used")
        idx_ok = sem("idx_ok")
        eb_ok = sem("eb_ok")
        g_in = [sem(f"g_in{j}") for j in range(GR)]
        gx_tr = sem("gx_tr")
        xh_ok = sem("xh_ok")
        xb_ok = sem("xb_ok")
        xl_ok = sem("xl_ok")
        h_mm = sem("h_mm")
        sg_ok = sem("sg_ok")
        y_ok = sem("y_ok")
        y_tr = sem("y_tr")
        yh_ok = sem("yh_ok")
        yl_ok = sem("yl_ok")
        yb_ok = sem("yb_ok")
        o_mm = sem("o_mm")
        ob_ok = sem("ob_ok")
        sc_out = sem("sc_out")

        block = ctx.enter_context(nc.Block())

        @block.sync
        def _(sp):
            sp.dma_start(X[:, 0:TB, :], x[0:S, :].rearrange("(t p) d -> p t d", p=P)).then_inc(x_in[0], 16)
            sp.dma_start(CT, ctxT.rearrange("(c p) n -> p c n", p=P)).then_inc(wts_in, 16)
            sp.dma_start(WQ[:], Wq.rearrange("(c p) n -> p c n", p=P)).then_inc(wts_in, 16)
            sp.dma_start(WKV[:], WkvT.rearrange("(c p) n -> p c n", p=P)).then_inc(wts_in, 16)
            sp.dma_start(WQT[:], WqT.rearrange("(c p) n -> p c n", p=P)).then_inc(wts_in, 16)
            sp.dma_start(WC[:], WcT.rearrange("(c p) n -> p c n", p=P)).then_inc(wts_in, 16)
            sp.dma_start(RT[:], routerT.rearrange("(c p) n -> p c n", p=P)).then_inc(wts_in, 16)
            sp.dma_start(X[:, TB:T, :], x[S:2 * S, :].rearrange("(t p) d -> p t d", p=P)).then_inc(x_in[1], 16)
            for e in range(E):
                sp.dma_start(raw[:, 2 + e * EC:2 + (e + 1) * EC, :], w[e * EC:(e + 1) * EC].rearrange("n p w -> p n w")
                             ).then_inc(raw_in[e], 16)
            sp.wait_ge(pad_ok, 1)
            sp.dma_start(rows[T * P:(T + 1) * P, :], xr[:, 0, :]).then_inc(rows_out, 16)
            sp.dma_start(out[T * P:(T + 1) * P, :], xr[:, 0, 0:D]).then_inc(rows_out, 16)
            def keep_residual(v):
                sp.wait_ge(x2_ok, v * 2 + 2)
                sp.dma_start(out[ds(v * (HT * P), HT * P), :].rearrange("(t p) d -> p t d", p=P),
                             X[:, ds(v * HT, HT), :]).then_inc(x2_out, 16)

            def keep_rows(v):
                sp.wait_ge(rows_ok, v + 1)
                sp.dma_start(rows[ds(v * (HT * P), HT * P), :].rearrange("(t p) d -> p t d", p=P),
                             xr[:]).then_inc(rows_out, 16)

            with sp.Fori(0, NH - 1) as v:
                keep_residual(v)
                keep_rows(v)
            for j in range(2):
                sp.wait_ge(low_out[j], 16 * NC // 2)
            sp.wait_ge(l2_mm, NH * NP)
            for e in range(E):
                sp.dma_start(W1lo[:, e * WC1:(e + 1) * WC1, :],
                             lows[e * EC:e * EC + WC1].rearrange("n p w -> p n w")).then_inc(low_in, 16)
            keep_residual(NH - 1)
            sp.wait_ge(x2_out, 16 * NH)
            sp.wait_ge(xn2_ok, T)
            for e in range(E):
                sp.dma_start(W2lo[:, e * WC2:(e + 1) * WC2, :],
                             lows[e * EC + WC1:(e + 1) * EC].rearrange("n p w -> p n w")).then_inc(low_in, 16)
            keep_rows(NH - 1)

        @block.gpsimd
        def _(pool):
            def iota(t, pattern, mult=0, start=0):
                pool.iota(t, pattern=pattern, base=start, channel_multiplier=mult,
                          allow_small_or_imprecise_dtypes=True).then_inc(iotas, 1)

            iota(iota_f[:], [[1, P]])
            iota(iota_p[:], [[0, 1]], 1)
            iota(iota_h[:], [[1, P]])
            iota(blk_h[:], [[1, BLK]])
            iota(blk_f[:], [[1, BLK]])
            iota(tok_h[:], [[P, T]], 1, 1)
            iota(k128[:], [[P, T]])
            iota(desc[:], [[-1, NK]], 0, NK)
            iota(desc_e[:], [[-1, E]], 0, E)
            iota(cum[:], [[1, E], [-1, E]])
            iota(spare[:], [[0, 1]], 1, T * P + 1)
            pool.memset(half[:], -0.5).then_inc(iotas, 1)
            pool.wait_ge(iotas, 12)
            for b in range(B):
                pool.wait_ge(ln_v, b + 1)
                pool.tensor_tensor(rs[:, b * TB:(b + 1) * TB], rs[:, b * TB:(b + 1) * TB], half[:, 0:TB], ALU.pow
                                   ).then_inc(ln_r, 1)


            def split(i, j, first):
                n = i * 2 + j
                pool.wait_ge(iotas, 12)
                pool.wait_ge(hi_ok, n + 1)
                if not first:
                    pool.wait_ge(low_out[j], i * 16)
                if first:
                    was, high = raw[:, n + 2, :], W[:, n, :]
                else:
                    was, high = (a.rearrange("p a w -> p (a w)") for a in (raw[:, ds(n + 2, 1), :], W[:, ds(n, 1), :]))
                pool.tensor_tensor(low[:, j, :], was, high.bitcast(F32), ALU.subtract).then_inc(low_ok, 1)

            def splits(start, stop):
                with pool.Fori(start // 2, stop // 2) as i:
                    for j in range(2):
                        split(i, j, False)

            for j in range(2):
                split(0, j, True)
            done = 2
            for v in range(NH):
                until = min(NC, (v + 2) * SLOTS + P2_AT)
                if until > done:
                    splits(done, until)
                    done = until
                pool.wait_ge(v2_ok, v + 1)
                pool.tensor_tensor(rs2[:], rs2[:], half[:, 0:HT], ALU.pow).then_inc(rs2_ok, 1)

            pool.wait_ge(idx_ok, 1)
            pool.wait_ge(rows_out, 16 * (2 * B + 2))
            pool.wait_ge(x2_out, 16 * 2 * B)

            def at_rows(b):
                return bass.IndirectOffsetOnAxis(ap=idx[:, b:b + 1], axis=0)

            for b in range(BLK + GR):
                if b >= GR:
                    c = b - GR
                    pool.wait_ge(ob_ok, c + 1)
                    if c >= 1:
                        pool.wait_ge(sc_out, 16 * c)
                    pool.indirect_dma_start(out=out, out_offset=at_rows(c), in_=ob[:, c % GR, :], in_offset=None,
                                            compute_op=ALU.add).then_inc(sc_out, 16)
                if b < BLK:
                    pool.indirect_dma_start(out=xg[:, b % GR, :], out_offset=None, in_=rows, in_offset=at_rows(b)
                                            ).then_inc(g_in[b % GR], 16)
            pool.wait_ge(sc_out, 16 * BLK)

        @block.scalar
        def _(act):
            act.wait_ge(wts_in, 16 * 6)
            act.wait_ge(g_mm, 1)
            act.copy(GT[:], ps[:, 0, 0:2 * B * NK].rearrange("p (c b n) -> p c b n", c=DC, b=B)).then_inc(g_out, 1)
            act.wait_ge(ks_tr, 1)
            act.copy(bd0.rearrange("p b (o n) -> p b o n", o=2),
                     ps[:, 2, 0:4 * P].rearrange("p (b n) -> p b n", b=2 * B)[:, :, 0:NK]
                     .rearrange("p (b o) n -> p b o n", b=B)).then_inc(bd0_ok, 1)

            def score_rows(b, j):
                n = b * HT + j
                act.wait_ge(x_tr, n + 1)
                i = 2 * (j % 2)
                act.copy(xT[:, i:i + 2], ps[:, j % 2, :].rearrange("p (t c q) -> p t c q", t=2, c=DC)).then_inc(xT_ok, 1)

            def high(n):
                if 2 <= n < NC + 2:
                    act.wait_ge(low_ok, n - 1)
                    act.dma_start(lows[n - 2], low[:, n % 2, :]).then_inc(low_out[n % 2], 16)
                if n < NC:
                    if n % EC == 0:
                        act.wait_ge(raw_in[n // EC], 16)
                    act.copy(W[:, n, :], raw[:, n + 2, :]).then_inc(hi_ok, 1)

            def exps(u, p):
                n = u * NP + p
                act.wait_ge(l2_mm, n + 1)
                if n >= 4:
                    act.wait_ge(pv_mm, (n - 4) // 2 + 1)
                act.activation(pT[0:NK, 2 * (n % 4):2 * (n % 4) + 2, :], ps[0:NK, 0:2, :], ACT.Exp).then_inc(ex_ok, 1)

            def prep_turned(w, z):
                t, g = divmod(z, 2)
                act.wait_ge(q_tr, w * 2 * HT + z + 1)
                act.copy(qT[:, w % 2, 4 * g:4 * g + 4, t * P:(t + 1) * P],
                         ps[:, 5, :].rearrange("p (n q) -> p n q", q=P)).then_inc(qT_ok, 1)

            def prep(x_due, p_due):
                if x_due:
                    w, t = x_due
                    act.wait_ge(px_tr, w * HT + t + 1)
                    act.copy(xpT[:, t % 2], ps[:, 4, 0:D].rearrange("p (c q) -> p c q", c=DC)).then_inc(pxT_ok, 1)
                if p_due:
                    w, t = p_due
                    q = w * HT + t
                    act.wait_ge(q_mm, q + 1)
                    if q:
                        act.wait_ge(q_tr, 2 * q)
                    act.copy(qs[:].rearrange("p h (c w) -> p h c w", w=DH)[:, :, 0:4:3, :].bitcast(F32R),
                             ps[:, 4, 0:D].rearrange("p (h w) -> p h w", w=DH).unsqueeze(2)
                             .broadcast_to([P, H, 2, DH])).then_inc(q_hi, 1)

            def post(v, k):
                if k in (0, 1):
                    act.wait_ge(o_tr, 2 * v + k + 1)
                    act.copy(oT[:, 2 * k:2 * k + 2].rearrange("p t c q -> p (t c q)"), ps[:, 3, :]).then_inc(oT_ok, 1)
                if k in (5, 6):
                    act.wait_ge(x2_tr, 2 * v + k - 4)
                    act.copy(oT[:, 2 * (k - 5):2 * (k - 5) + 2].rearrange("p t c q -> p (t c q)"), ps[:, 3, :]
                             ).then_inc(x2T_ok, 1)
                if k == 8:
                    act.wait_ge(lm_ok, v + 1)
                    act.activation(ex[:], lm[:], ACT.Exp).then_inc(exr_ok, 1)

            for j in range(HT):
                score_rows(0, j)
            prep((0, 0), (0, 0))
            for u in range(-1, NH + 1):
                for p in range(SLOTS):
                    if u + 1 < NH and p < 2 * HT:
                        prep_turned(u + 1, p)
                    if 0 <= u < NH and 1 <= p <= NP:
                        exps(u, p - 1)
                    prep(due(X_AT, u, p), due(P_AT, u, p))
                    if u < 0 and p in SCORES_AT:
                        score_rows(1, SCORES_AT.index(p))
                    if u >= 1 and p:
                        post(u - 1, p - 1)
                    high((u + 1) * SLOTS + p)
                if u + 1 < NH:
                    act.wait_ge(mx_tr, u + 2)
                    act.copy(mT[:], ps[:, 5, :]).then_inc(mT_ok, 1)

            def rows_in(b):
                act.wait_ge(gx_tr, b + 1)
                act.copy(x_hi, ps[:, 2, 0:D]).then_inc(xh_ok, 1)
                act.wait_ge(xh_ok, b + 1)
                act.copy(x_b, x_hi.bitcast(F32)).then_inc(xb_ok, 1)

            def result(b, j, first):
                e = act.value_load(eb[0:1, ds(b, 1)], min_val=0, max_val=E - 1)
                act.wait_ge(o_mm, b + 1)
                if not first:
                    act.wait_ge(sc_out, (b - 2) * 16)
                act.activation(ob[:, j, :], ps[:, 4, 0:D], ACT.Copy, scale=xg[:, j, ds(e + D, 1)]).then_inc(ob_ok, 1)

            def step(i, first, last):
                for j in range(GR if not last else BLK - i * GR):
                    b = i * GR + j
                    act.wait_ge(h_mm, b + 1)
                    act.activation(sg, ps[:, 0, :], ACT.Silu).then_inc(sg_ok, 1)
                    if not (last and b == BLK - 1):
                        rows_in(b + 1)
                    if not (first and j == 0):
                        result(b - 1, (j - 1) % GR, first)
                    act.wait_ge(y_tr, b + 1)
                    act.copy(y_hi[:], ps[:, 3, :]).then_inc(yh_ok, 1)

            act.wait_ge(eb_ok, 1)
            rows_in(0)
            step(0, True, False)
            with act.Fori(1, LAST) as i:
                step(i, False, False)
            step(LAST, False, True)
            result(BLK - 1, (BLK - 1) % GR, False)

        @block.vector
        def _(dve):
            dve.wait_ge(iotas, 12)
            dve.tensor_scalar(ident[:], iota_f[:], iota_p[:, 0:1], None, ALU.is_equal).then_inc(consts, 1)
            dve.tensor_scalar(tri[:], iota_f[:], iota_p[:, 0:1], None, ALU.is_gt).then_inc(consts, 1)
            dve.memset(ones[:], 1.0).then_inc(consts, 1)
            dve.tensor_scalar(sel_e[:], iota_p[:], float(ONE), None, ALU.is_equal).then_inc(consts, 1)
            dve.tensor_scalar(sel_o[:], iota_p[:], float(HS + ONE), None, ALU.is_equal).then_inc(consts, 1)
            dve.tensor_scalar(neg[:], iota_f[:, 0:H], iota_p[:, 0:1], -1.0, ALU.is_equal, ALU.mult).then_inc(consts, 1)
            dve.tensor_scalar(lt8[:], cum[:], 0.0, None, ALU.is_ge).then_inc(consts, 1)

            def variances(b):
                dve.wait_ge(ln_st, (b + 1) * TB)
                for t in range(b * TB, (b + 1) * TB):
                    dve.bn_aggr(mv[:, t, :], st[:, t, :]).then_inc(ln_mv, 1)
                dve.wait_ge(ln_mv, (b + 1) * TB)
                dve.tensor_scalar(rs[:, b * TB:(b + 1) * TB], mv[:, b * TB:(b + 1) * TB, 1], EPS, None, ALU.add
                                  ).then_inc(ln_v, 1)

            dve.wait_ge(x_in[0], 16)
            for t in range(TB):
                dve.bn_stats(st[:, t, :], X[:, t, :]).then_inc(ln_st, 1)
            variances(0)
            dve.memset(ks, 0.0).then_inc(consts, 1)
            dve.memset(qs[:], 0.0).then_inc(consts, 1)
            dve.memset(mx[:], 0.0).then_inc(consts, 1)
            dve.memset(vc[:], 0.0).then_inc(consts, 1)
            dve.wait_ge(consts, 11)
            dve.memset(qs[:, :, ONE:ONE + 1], 1.0).then_inc(consts, 1)
            dve.wait_ge(kv_mm, 1)
            kv = ps[0:NK, 1, 0:B * 2 * DH].rearrange("p (b n) -> p b n", b=B)
            for b in range(B):
                for o in range(2):
                    for at in (HI_A, LO_A):
                        dve.tensor_scalar(ks[:, b, o, o * HS + at:o * HS + at + DH].bitcast(F32R),
                                          kv[:, b, 0:DH], SCALE, None, ALU.mult).then_inc(ks_hi, 1)
            dve.tensor_copy(mvb[:], kv[:, :, DH:2 * DH]).then_inc(ks_ok, 1)
            dve.wait_ge(ks_hi, 4 * B)
            for b in range(B):
                for o in range(2):
                    dve.scalar_tensor_tensor(ks[:, b, o, o * HS + HI_B:o * HS + HI_B + DH], kv[:, b, 0:DH], SCALE,
                                             ks[:, b, o, o * HS:o * HS + DH], ALU.mult, ALU.subtract
                                             ).then_inc(ks_ok, 1)
            dve.wait_ge(bd0_ok, 1)
            dve.wait_ge(consts, 12)

            def score_rows(b, j):
                if j >= 2:
                    dve.wait_ge(x_tr, b * HT + j - 1)
                for t in range(2 * j, 2 * j + 2):
                    q = b * TB + t
                    dve.tensor_scalar(xn[:, t % HT, :], X[:, q, :], mv[:, q, 0:1], rs[:, q:q + 1],
                                      ALU.subtract, ALU.mult).then_inc(xn_ok, 1)

            def scores(b, j):
                n = b * HT + j
                dve.wait_ge(q_sc, n + 1)
                dve.tensor_copy(sc[:, 2 * n:2 * n + 2, :], ps[:, 2, 0:2 * NK].rearrange("p (t n) -> p t n", n=NK)
                                ).then_inc(sc_ok, 1)

            def picks(b):
                here = slice(b * TB, (b + 1) * TB)
                dve.wait_ge(sc_ok, (b + 1) * HT)
                dve.tensor_reduce(m1[:, here], sc[:, here], AX.X, ALU.max).then_inc(am, 1)
                dve.wait_ge(am, 4 * b + 1)
                dve.tensor_tensor(eqw[:, here], sc[:, here], m1[:, here].unsqueeze(2).broadcast_to([P, TB, NK]),
                                  ALU.is_equal).then_inc(am, 1)
                dve.wait_ge(am, 4 * b + 2)
                dve.tensor_tensor(eqw[:, here], eqw[:, here], desc[:].unsqueeze(1).broadcast_to([P, TB, NK]), ALU.mult
                                  ).then_inc(am, 1)
                dve.wait_ge(am, 4 * b + 3)
                dve.tensor_reduce(m2[:, here], eqw[:, here], AX.X, ALU.max).then_inc(am, 1)
                dve.wait_ge(am, 4 * b + 4)
                dve.tensor_tensor(oh[:, here], eqw[:, here], m2[:, here].unsqueeze(2).broadcast_to([P, TB, NK]),
                                  ALU.is_equal).then_inc(oh_ok, 1)

            def masks(b):
                dve.wait_ge(cnt_mm, b + 1)
                dve.tensor_scalar(bias[:, b, :], ps[:, 3, 0:NK], 0.5, MASK, ALU.is_lt, ALU.mult).then_inc(cnt_ok, 1)
                dve.tensor_copy(cc[:, b:b + 1], ps[0:NK, 3, NK:NK + 1]).then_inc(cnt_ok, 1)
                dve.wait_ge(cnt_ok, 2 * b + 2)
                for o, sel in enumerate((sel_e, sel_o)):
                    dve.scalar_tensor_tensor(bd[:, b, o * NK:(o + 1) * NK], bias[:, b, :], sel[:, 0:1],
                                             bd0[:, b, o * NK:(o + 1) * NK], ALU.mult, ALU.add).then_inc(bd_ok, 1)
                dve.tensor_scalar(vc[:, b, 0:DH], mvb[:, b, :], cc[:, b:b + 1], None, ALU.mult).then_inc(bd_ok, 1)
                dve.tensor_copy(vc[:, b, DH:DH + 1], cc[:, b:b + 1]).then_inc(bd_ok, 1)

            def normalise(w, t):
                q = w * HT + t
                if q >= 2:
                    dve.wait_ge(px_tr, q - 1)
                dve.tensor_scalar(xp[:, t % 2, :], X[:, q, :], mv[:, q, 0:1], rs[:, q:q + 1],
                                  ALU.subtract, ALU.mult).then_inc(xp_ok, 1)

            def prep_low(w, t):
                dve.wait_ge(q_hi, w * HT + t + 1)
                dve.tensor_tensor(qs[:, :, LO_A:LO_A + DH].bitcast(F32R), ps[:, 4, 0:D].rearrange("p (h w) -> p h w", w=DH),
                                  qs[:, :, HI_A:HI_A + DH], ALU.subtract).then_inc(q_lo, 1)

            def maxima(w, z):
                t, g = divmod(z, 2)
                dve.wait_ge(l1_mm, w * 2 * HT + z + 1)
                if w and not z:
                    dve.wait_ge(mx_tr, w)
                dve.tensor_reduce(mx[:, t * H + g * 8:t * H + g * 8 + 8],
                                  ps[:, 6:8, 0:4 * NK].rearrange("p k (h n) -> p k h n", n=NK),
                                  AX.X, ALU.max).then_inc(mx_ok, 1)

            def post(v, k):
                here = slice(v * HT, (v + 1) * HT)
                if k in (2, 3):
                    g = k - 2
                    dve.wait_ge(wc_mm, 2 * v + g + 1)
                    xv = X[:, v * HT + 2 * g:v * HT + 2 * g + 2, :]
                    dve.tensor_tensor(xv, xv, ps[:, 3, :].rearrange("p (t d) -> p t d", d=D), ALU.add
                                      ).then_inc(x2_ok, 1)
                    dve.wait_ge(x2_ok, 2 * v + g + 1)
                    for i in range(2 * g, 2 * g + 2):
                        dve.bn_stats(st2[:, i, :], X[:, v * HT + i, :]).then_inc(st2_ok, 1)
                    for i in range(2 * g, 2 * g + 2):
                        dve.wait_ge(st2_ok, v * HT + i + 1)
                        dve.bn_aggr(mv2[:, i, :], st2[:, i, :]).then_inc(mv2_ok, 1)
                if k == 3:
                    dve.wait_ge(mv2_ok, v * HT + HT)
                    dve.tensor_scalar(rs2[:], mv2[:, :, 1], EPS, None, ALU.add).then_inc(v2_ok, 1)
                if k == 4:
                    dve.wait_ge(rs2_ok, v + 1)
                    dve.wait_ge(rows_out, 32 + 16 * v)
                    for i in range(HT):
                        dve.tensor_scalar(xn2[:, i, :], X[:, v * HT + i, :],
                                          mv2[:, i, 0:1], rs2[:, i:i + 1], ALU.subtract, ALU.mult).then_inc(xn2_ok, 1)
                if k not in (7, 8, 9):
                    return
                wide = lambda a: a.unsqueeze(2).broadcast_to([P, HT, E])
                dese = desc_e[:].unsqueeze(1).broadcast_to([P, HT, E])
                steps = 14
                done = [{7: 0, 8: 4, 9: 11}[k]]

                def link(ins):
                    done[0] += 1
                    ins.then_inc(top, 1)
                    dve.wait_ge(top, v * steps + done[0])

                if k == 7:
                    dve.wait_ge(r_mm, v + 1)
                    link(dve.tensor_copy(rl[:], ps[:, 3, 0:HT * E].rearrange("p (t e) -> p t e", e=E)))
                    link(dve.tensor_reduce(r1[:], rl[:], AX.X, ALU.max))
                    dve.tensor_tensor(lm[:], rl[:], wide(r1[:]), ALU.subtract).then_inc(lm_ok, 1)
                    link(dve.tensor_tensor(eq[:], rl[:], wide(r1[:]), ALU.is_equal))
                    link(dve.tensor_tensor(eq[:], eq[:], dese, ALU.mult))
                if k == 8:
                    link(dve.tensor_reduce(f1[:], eq[:], AX.X, ALU.max))
                    link(dve.tensor_tensor(o1[:, here, :], eq[:], wide(f1[:]), ALU.is_equal))
                    link(dve.scalar_tensor_tensor(rl[:], o1[:, here, :], -1e38, rl[:], ALU.mult, ALU.add))
                    link(dve.tensor_reduce(r1[:], rl[:], AX.X, ALU.max))
                    link(dve.tensor_tensor(eq[:], rl[:], wide(r1[:]), ALU.is_equal))
                    link(dve.tensor_tensor(eq[:], eq[:], dese, ALU.mult))
                    link(dve.tensor_reduce(f1[:], eq[:], AX.X, ALU.max))
                    dve.tensor_tensor(o2[:, here, :], eq[:], wide(f1[:]), ALU.is_equal).then_inc(rl_ok, 1)
                if k == 9:
                    dve.wait_ge(rl_ok, v + 1)
                    dve.tensor_tensor(cnt[:, here, :], o1[:, here, :], o2[:, here, :], ALU.add).then_inc(cnt_s, 1)
                    dve.wait_ge(exr_ok, v + 1)
                    link(dve.tensor_reduce(sme[:], ex[:], AX.X, ALU.add))
                    link(dve.reciprocal(sme[:], sme[:]))
                    dve.wait_ge(cnt_s, v + 1)
                    link(dve.tensor_tensor(ex[:], ex[:], cnt[:, here, :], ALU.mult))
                    dve.tensor_tensor(xr[:, :, D:RW], ex[:], wide(sme[:]), ALU.mult).then_inc(rows_ok, 1)

            def sums(u, p):
                if p % 2 == 0 and p >= 2:
                    n = u * NG + p // 2 - 1
                    dve.wait_ge(pv_mm, n + 1)
                    if n >= 2:
                        dve.wait_ge(tu_mm, n - 1)
                    dve.tensor_copy(uT[:, n % 2, :], ps[:, 2, :]).then_inc(ut_ok, 1)
                if p % 2 == 1 and p >= 3:
                    g = (p - 3) // 2
                    n = u * NG + g
                    dve.wait_ge(tu_mm, n + 1)
                    if u and g == 0:
                        dve.wait_ge(o_tr, 2 * u)
                    uv = ps[:, 2, :].rearrange("p (t h w) -> p t h w", h=4, w=UH)
                    dve.reciprocal(rden[:], uv[:, :, :, DH]).then_inc(rd_ok, 1)
                    dve.wait_ge(rd_ok, n + 1)
                    dve.tensor_tensor(on[:].rearrange("p t (h w) -> p t h w", w=DH)[:, :, 4 * g:4 * g + 4, :],
                                      uv[:, :, :, 0:DH], rden[:].unsqueeze(3).broadcast_to([P, HT, 4, DH]), ALU.mult
                                      ).then_inc(on_ok, 1)

            dve.wait_ge(ln_r, 1)
            score_rows(0, 0)
            score_rows(0, 1)
            for j in range(HT):
                if j + 2 < HT:
                    score_rows(0, j + 2)
                scores(0, j)
                if j == 0:
                    dve.wait_ge(x_in[1], 16)
                for t in range(TB + 2 * j, TB + 2 * j + 2):
                    dve.bn_stats(st[:, t, :], X[:, t, :]).then_inc(ln_st, 1)
            variances(1)
            normalise(0, 0)
            picks(0)
            normalise(0, 1)
            prep_low(0, 0)
            for u in range(-1, NH + 1):
                for p in range(SLOTS):
                    if u < 0:
                        if p == 0:
                            dve.memset(xr[:], 0.0).then_inc(pad_ok, 1)
                        if p == MASKS_AT[0]:
                            masks(0)
                            dve.wait_ge(ln_r, B)
                        if p in SCORES_AT:
                            score_rows(1, SCORES_AT.index(p))
                    if u + 1 < NH and 1 <= p <= 2 * HT:
                        maxima(u + 1, p - 1)
                    if u >= 1 and p == 0:
                        sums(u - 1, SLOTS - 1)
                    if 0 <= u < NH and p:
                        sums(u, p - 1)
                    if due(P_AT, u, p):
                        prep_low(*due(P_AT, u, p))
                    if due(XN_AT, u, p):
                        normalise(*due(XN_AT, u, p))
                    if u < 0 and p - 1 in SCORES_AT:
                        scores(1, SCORES_AT.index(p - 1))
                    if u < 0 and p == PICKS_AT:
                        picks(1)
                    if u < 0 and p == MASKS_AT[1]:
                        masks(1)
                    if u >= 2 and p == 0:
                        post(u - 2, SLOTS - 1)
                    if u >= 1 and p:
                        post(u - 1, p - 1)
            post(NH - 1, SLOTS - 1)

            links = [0]

            def link(ins):
                links[0] += 1
                ins.then_inc(rt, 1)
                dve.wait_ge(rt, links[0])

            dve.wait_ge(pre_mm, 1)
            link(dve.tensor_tensor(ce, ps[:, 1, 0:E].unsqueeze(2).broadcast_to([P, E, T]),
                                   k128[:].unsqueeze(1).broadcast_to([P, E, T]), ALU.is_gt))
            link(dve.tensor_reduce(nb[:], ce, AX.X, ALU.add))
            link(dve.tensor_tensor(cum[:], lt8[:], nb[:].unsqueeze(1).broadcast_to([P, E, E]), ALU.mult))
            link(dve.tensor_reduce(end[:], cum[:], AX.X, ALU.add))
            link(dve.tensor_tensor(base[:], end[:], nb[:], ALU.subtract))
            link(dve.tensor_scalar(base[:], base[:], float(P), None, ALU.mult))
            link(dve.tensor_tensor(slf, ps[:, 0, 0:T * E].rearrange("p (t e) -> p t e", e=E),
                                   base[:].unsqueeze(1).broadcast_to([P, T, E]), ALU.add))
            for k, o in enumerate((o1, o2)):
                link(dve.tensor_tensor(pick, slf, o[:], ALU.mult))
                link(dve.tensor_reduce(slot[:, k, :], pick, AX.X, ALU.add))
            link(dve.tensor_copy(sloti[:], slot[:].rearrange("p k t -> p (k t)")))
            link(dve.tensor_scalar(bki[:], sloti[:], 7, None, ALU.logical_shift_right))
            link(dve.tensor_scalar(rmi[:], sloti[:], P - 1, None, ALU.bitwise_and))
            link(dve.tensor_copy(bkh[:], bki[:]))
            link(dve.tensor_copy(rmh[:], rmi[:]))
            link(dve.tensor_tensor(bsel, blk_h[:].unsqueeze(1).broadcast_to([P, 2 * T, BLK]),
                                   bkh[:].unsqueeze(2).broadcast_to([P, 2 * T, BLK]), ALU.is_equal))
            for k in range(2):
                link(dve.tensor_tensor(bval[:, k * T:(k + 1) * T, :], bsel[:, k * T:(k + 1) * T, :],
                                       tok_h[:].unsqueeze(2).broadcast_to([P, T, BLK]), ALU.mult))

            for n in range(0, 2 * T, 8):
                dve.tensor_tensor(asel[:, n:n + 8, :], iota_h[:].unsqueeze(1).broadcast_to([P, 8, P]),
                                  rmh[:, n:n + 8].unsqueeze(2).broadcast_to([P, 8, P]), ALU.is_equal
                                  ).then_inc(asel_ok, 1)
            dve.wait_ge(asel_used, 1)
            link(dve.tensor_copy(tokp[:], ps[:, 2, 0:BLK]))
            link(dve.tensor_scalar(idf[:], tokp[:], 0.0, spare[:, 0:1], ALU.is_equal, ALU.mult))
            dve.scalar_tensor_tensor(idx[:], tokp[:], -1.0, idf[:], ALU.add, ALU.add).then_inc(idx_ok, 1)
            link(dve.tensor_tensor(ebc, blk_f[:].unsqueeze(2).broadcast_to([P, BLK, E]),
                                   end[:].unsqueeze(1).broadcast_to([P, BLK, E]), ALU.is_ge))
            link(dve.tensor_reduce(ebf[:], ebc, AX.X, ALU.add))
            dve.tensor_scalar(eb[:], ebf[:], float(E - 1), None, ALU.min).then_inc(eb_ok, 1)

            def rows_low(b):
                dve.wait_ge(xh_ok, b + 1)
                dve.tensor_tensor(x_lo, ps[:, 2, 0:D], x_hi.bitcast(F32), ALU.subtract).then_inc(xl_ok, 1)

            def step(i, blocks, last):
                for j in range(blocks):
                    b = i * GR + j
                    dve.wait_ge(sg_ok, b + 1)
                    dve.tensor_tensor(yb, sg, ps[:, 1, :], ALU.mult).then_inc(y_ok, 1)
                    if not (last and j == blocks - 1):
                        rows_low(b + 1)
                    dve.wait_ge(yh_ok, b + 1)
                    dve.tensor_tensor(y_lo, ps[:, 3, :], y_hi[:].bitcast(F32), ALU.subtract).then_inc(yl_ok, 1)
                    dve.tensor_copy(y_b, y_hi[:].bitcast(F32)).then_inc(yb_ok, 1)

            rows_low(0)
            with dve.Fori(0, LAST) as i:
                step(i, GR, False)
            step(LAST, BLK - LAST * GR, True)

        @block.tensor
        def _(pe):
            pe.wait_ge(wts_in, 16 * 6)
            for c in range(DC):
                for k in range(DC):
                    mm = pe.matmul(ps[:, 0, c * B * NK:(c + 1) * B * NK], WQ[:, k, c * P:(c + 1) * P], CT[:, k, :],
                                   start=(k == 0), stop=(k == DC - 1))
            mm.then_inc(g_mm, 1)
            for b in range(B):
                for k in range(DC):
                    mm = pe.matmul(ps[0:NK, 1, b * 2 * DH:(b + 1) * 2 * DH], CT[:, k, b * NK:(b + 1) * NK], WKV[:, k, :],
                                   start=(k == 0), stop=(k == DC - 1))
            mm.then_inc(kv_mm, 1)
            pe.wait_ge(consts, 12)
            pe.wait_ge(ks_ok, 2 * B + 1)
            for n in range(2 * B):
                mm = pe.transpose(ps[:, 2, n * P:n * P + NK], ks[:, n // 2, n % 2, :], ident[0:NK, 0:NK])
            mm.then_inc(ks_tr, 1)
            pe.wait_ge(g_out, 1)
            pe.wait_ge(bd0_ok, 1)

            def score_turn(b, j):
                pe.wait_ge(xn_ok, b * TB + 2 * j + 2)
                if b or j >= 2:
                    pe.wait_ge(xT_ok, b * HT + j - 1)
                for t in range(2):
                    for c in range(DC):
                        mm = pe.transpose(ps[:, j % 2, (t * DC + c) * P:(t * DC + c + 1) * P],
                                          xn[:, 2 * (j % 2) + t, c * P:(c + 1) * P], ident[:])
                mm.then_inc(x_tr, 1)

            def score(b, j):
                n = b * HT + j
                pe.wait_ge(xT_ok, n + 1)
                if n:
                    pe.wait_ge(sc_ok, n)
                for t in range(2):
                    for c in range(DC):
                        mm = pe.matmul(ps[:, 2, t * NK:(t + 1) * NK], xT[:, 2 * (j % 2) + t, c, :], GT[:, c, b, :],
                                       start=(c == 0), stop=(c == DC - 1))
                mm.then_inc(q_sc, 1)

            def counts(b):
                pe.wait_ge(oh_ok, b + 1)
                if b:
                    pe.wait_ge(cnt_ok, 2 * b)
                for t in range(b * TB, (b + 1) * TB):
                    pe.matmul(ps[:, 3, 0:NK], ones[:], oh[:, t, :], start=(t % TB == 0), stop=(t % TB == TB - 1))
                for t in range(b * TB, (b + 1) * TB):
                    mm = pe.matmul(ps[0:NK, 3, NK:NK + 1], oh[:, t, :], ones[:, 0:1],
                                   start=(t % TB == 0), stop=(t % TB == TB - 1))
                mm.then_inc(cnt_mm, 1)

            def prep_x(w, t):
                q = w * HT + t
                pe.wait_ge(xp_ok, q + 1)
                if q:
                    pe.wait_ge(q_lo, q)
                for c in range(DC):
                    mm = pe.transpose(ps[:, 4, c * P:(c + 1) * P], xp[:, t % 2, c * P:(c + 1) * P], ident[:])
                mm.then_inc(px_tr, 1)

            def prep_project(w, t):
                q = w * HT + t
                pe.wait_ge(pxT_ok, q + 1)
                for c in range(DC):
                    mm = pe.matmul(ps[:, 4, 0:D], xpT[:, t % 2, c, :], WQT[:, c, :], start=(c == 0), stop=(c == DC - 1))
                mm.then_inc(q_mm, 1)

            def prep_turn(w, z):
                t, g = divmod(z, 2)
                pe.wait_ge(q_lo, w * HT + t + 1)
                if w or z:
                    pe.wait_ge(qT_ok, w * 2 * HT + z)
                if w and z == 0:
                    pe.wait_ge(mT_ok, w)
                for n in range(4):
                    a = 2 * (4 * g + n)
                    mm = pe.transpose(ps[:, 5, n * P:(n + 1) * P], qs[:, a:a + 2, :].rearrange("p h w -> p (h w)"),
                                      ident[:])
                mm.then_inc(q_tr, 1)

            def prep_logits(w, z):
                t, g = divmod(z, 2)
                if w % 2 == 0 and z == 0:
                    pe.wait_ge(bd_ok, 4 * (w // 2 + 1))
                pe.wait_ge(qT_ok, w * 2 * HT + z + 1)
                if w or z:
                    pe.wait_ge(mx_ok, w * 2 * HT + z)
                for n in range(4):
                    mm = pe.matmul(ps[:, 6 + n // 2, (n % 2) * 2 * NK:(n % 2 + 1) * 2 * NK],
                                   qT[:, w % 2, 4 * g + n, t * P:(t + 1) * P], bd[:, w // 2, :], start=True, stop=True)
                mm.then_inc(l1_mm, 1)

            def prep_maxima(w):
                pe.wait_ge(mx_ok, (w + 1) * 2 * HT)
                pe.wait_ge(qT_ok, (w + 1) * 2 * HT)
                for i in range(HT):
                    mm = pe.transpose(ps[:, 5, i * P:(i + 1) * P], mx[:, i * H:i * H + P], ident[:])
                mm.then_inc(mx_tr, 1)

            def logits(u, p):
                n = u * NP + p
                if p == 0:
                    pe.wait_ge(mT_ok, u + 1)
                if n:
                    pe.wait_ge(ex_ok, n)
                for o in range(2):
                    pe.matmul(ps[0:NK, o, :], bd[:, u // 2, o * NK:(o + 1) * NK], qT[:, u % 2, p, :],
                              start=True, stop=False)
                    mm = pe.matmul(ps[0:NK, o, :], neg[:, 2 * p + o:2 * p + o + 1].broadcast_to([P, NK]), mT[:],
                                   start=False, stop=True)
                mm.then_inc(l2_mm, 1)

            def sums(u, p):
                if p % 2 == 0 and p >= 2:
                    g = p // 2 - 1
                    n = u * NG + g
                    pe.wait_ge(ex_ok, u * NP + 2 * g + 2)
                    if n:
                        pe.wait_ge(on_ok, n)
                    for h in range(4):
                        mm = pe.matmul(ps[h * UH:(h + 1) * UH, 2, :], vc[:, u // 2, :], pT[0:NK, 4 * (n % 2) + h, :],
                                       start=True, stop=True)
                    mm.then_inc(pv_mm, 1)
                if p % 2 == 1 and p >= 3:
                    n = u * NG + (p - 3) // 2
                    pe.wait_ge(ut_ok, n + 1)
                    for i in range(HT):
                        mm = pe.transpose(ps[:, 2, i * P:(i + 1) * P], uT[:, n % 2, i * P:(i + 1) * P], ident[:])
                    mm.then_inc(tu_mm, 1)

            def turn(src, g, done):
                for i in range(2 * g, 2 * g + 2):
                    for c in range(DC):
                        mm = pe.transpose(ps[:, 3, ((i % 2) * DC + c) * P:((i % 2) * DC + c + 1) * P],
                                          src[:, i, c * P:(c + 1) * P], ident[:])
                mm.then_inc(done, 1)

            def post(v, k):
                if k == 0:
                    pe.wait_ge(on_ok, (v + 1) * NG)
                    turn(on, 0, o_tr)
                if k == 1:
                    pe.wait_ge(oT_ok, 2 * v + 1)
                    turn(on, 1, o_tr)
                if k in (2, 3):
                    g = k - 2
                    pe.wait_ge(oT_ok, 2 * v + 2)
                    if g:
                        pe.wait_ge(x2_ok, 2 * v + 1)
                    for i in range(2 * g, 2 * g + 2):
                        for c in range(DC):
                            mm = pe.matmul(ps[:, 3, (i % 2) * D:(i % 2 + 1) * D], oT[:, i, c, :], WC[:, c, :],
                                           start=(c == 0), stop=(c == DC - 1))
                    mm.then_inc(wc_mm, 1)
                if k == 5:
                    pe.wait_ge(xn2_ok, (v + 1) * HT)
                    turn(xn2, 0, x2_tr)
                if k == 6:
                    pe.wait_ge(x2T_ok, 2 * v + 1)
                    turn(xn2, 1, x2_tr)
                if k == 7:
                    pe.wait_ge(x2T_ok, 2 * v + 2)
                    for i in range(HT):
                        for c in range(DC):
                            mm = pe.matmul(ps[:, 3, i * E:(i + 1) * E], oT[:, i, c, :], RT[:, c, :],
                                           start=(c == 0), stop=(c == DC - 1))
                    mm.then_inc(r_mm, 1)

            score_turn(0, 0)
            for j in range(HT):
                if j + 1 < HT:
                    score_turn(0, j + 1)
                score(0, j)
            prep_x(0, 0)
            prep_project(0, 0)
            for u in range(-1, NH + 1):
                prepares = u + 1 < NH
                for p in range(SLOTS):
                    if prepares and p < 2 * HT:
                        prep_turn(u + 1, p)
                    if u < 0 and p in MASKS_AT:
                        counts(MASKS_AT.index(p))
                    if 0 <= u < NH and 1 <= p <= NP:
                        logits(u, p - 1)
                    if prepares and 1 <= p <= 2 * HT:
                        prep_logits(u + 1, p - 1)
                    if u >= 1 and p == 0:
                        sums(u - 1, SLOTS - 1)
                    if 0 <= u < NH and p:
                        sums(u, p - 1)
                    if due(X_AT, u, p):
                        prep_x(*due(X_AT, u, p))
                    if due(P_AT, u, p):
                        prep_project(*due(P_AT, u, p))
                    if u < 0 and p - 1 in SCORES_AT:
                        score(1, SCORES_AT.index(p - 1))
                    if u < 0 and p in SCORES_AT:
                        score_turn(1, SCORES_AT.index(p))
                    if u >= 1 and p:
                        post(u - 1, p - 1)
                if prepares:
                    prep_maxima(u + 1)

            pe.wait_ge(cnt_s, NH)
            pe.matmul(ps[:, 0, 0:T * E], tri[:], cnt[:].rearrange("p t e -> p (t e)"), start=True, stop=False)
            for t in range(T - 1):
                pe.matmul(ps[:, 0, (t + 1) * E:T * E].rearrange("p (t e) -> p t e", e=E), ones[:],
                          cnt[:, t, :].unsqueeze(1).broadcast_to([P, T - 1 - t, E]), start=False, stop=(t == T - 2))
            for t in range(T):
                mm = pe.matmul(ps[:, 1, 0:E], ones[:], cnt[:, t, :], start=(t == 0), stop=(t == T - 1))
            mm.then_inc(pre_mm, 1)
            for n in range(2 * T):
                if n % 8 == 0:
                    pe.wait_ge(asel_ok, n // 8 + 1)
                mm = pe.matmul(ps[:, 2, 0:BLK], asel[:, n, :], bval[:, n, :], start=(n == 0), stop=(n == 2 * T - 1))
            mm.then_inc(asel_used, 1)

            pe.wait_ge(hi_ok, NC)
            pe.wait_ge(low_in, 16 * 2 * E)
            pe.wait_ge(eb_ok, 1)
            pe.wait_ge(idx_ok, 1)

            def turn_rows(j, value):
                pe.wait_ge(g_in[j], value)
                for c in range(DC):
                    mm = pe.transpose(ps[:, 2, c * P:(c + 1) * P], xg[:, j, c * P:(c + 1) * P], ident[:])
                mm.then_inc(gx_tr, 1)

            def chunk(t, n):
                return t[:, ds(n, 1), :].rearrange("p a w -> p (a w)")

            def inner(b, e):
                pe.wait_ge(xh_ok, b + 1)
                pe.wait_ge(xl_ok, b + 1)
                pe.wait_ge(xb_ok, b + 1)
                for k, (part, wts, per) in enumerate(((x_hi, W, EC), (x_lo, W, EC), (x_b, W1lo, WC1))):
                    for c in range(DC):
                        for f in range(2):
                            mm = pe.matmul(ps[:, f, :], part[:, c * P:(c + 1) * P], chunk(wts, e * per + (2 * c + f)),
                                           start=(k == 0 and c == 0), stop=(k == 2 and c == DC - 1))
                mm.then_inc(h_mm, 1)

            def outer(b, e):
                pe.wait_ge(yh_ok, b + 1)
                pe.wait_ge(yl_ok, b + 1)
                pe.wait_ge(yb_ok, b + 1)
                for k, (part, wts, per, at) in enumerate(((y_hi, W, EC, WC1), (y_lo, W, EC, WC1), (y_b, W2lo, WC2, 0))):
                    for c in range(FC):
                        w2 = chunk(wts, e * per + (at + c // 2))[:, (c % 2) * D:(c % 2 + 1) * D]
                        mm = pe.matmul(ps[:, 4, 0:D], part[:, c * P:(c + 1) * P], w2,
                                       start=(k == 0 and c == 0), stop=(k == 2 and c == FC - 1))
                mm.then_inc(o_mm, 1)

            def turn_y(b):
                pe.wait_ge(y_ok, b + 1)
                for c in range(FC):
                    mm = pe.transpose(ps[:, 3, c * P:(c + 1) * P], yb[:, c * P:(c + 1) * P], ident[:])
                mm.then_inc(y_tr, 1)

            def expert(b):
                return pe.value_load(eb[0:1, ds(b, 1)], min_val=0, max_val=E - 1)

            def step(i, first, last):
                e_last = e = None
                blocks = BLK - i * GR if last else GR
                for j in range(blocks):
                    b = i * GR + j
                    final = last and j == blocks - 1
                    if not final:
                        turn_rows((j + 1) % GR, i * 16 + (16 if j < GR - 1 else 32))
                    if j == 0 and not first:
                        e_last = expert(b - 1)
                    e_next = expert(b + 1) if j and not final else None
                    if not (first and j == 0):
                        if not (first and j == 1):
                            pe.wait_ge(ob_ok, b - 1)
                        outer(b - 1, e_last)
                    if j == 0:
                        e = expert(b)
                        e_next = None if final else expert(b + 1)
                    turn_y(b)
                    if not final:
                        inner(b + 1, e_next)
                    e_last, e = e, e_next
                return e_last

            turn_rows(0, 16)
            inner(0, expert(0))
            step(0, True, False)
            with pe.Fori(1, LAST) as i:
                step(i, False, False)
            e = step(LAST, False, True)
            pe.wait_ge(ob_ok, BLK - 1)
            outer(BLK - 1, e)


def kernel(x, ctx_1024, L0_xattn_Wq, L0_xattn_Wkv, L0_xattn_Wc, L0_ffn_w1, L0_ffn_w2, L0_ffn_router_w):
    import numpy as np
    from concourse import bacc
    from concourse.bass_utils import run_bass_kernel_spmd

    nc = bacc.Bacc("TRN2", target_bir_lowering=False, num_devices=1)
    laid = {
        "x": np.asarray(x).reshape(B * S, D),
        "ctxT": np.asarray(ctx_1024).reshape(B * NK, D).T,
        "Wq": np.asarray(L0_xattn_Wq),
        "WqT": np.asarray(L0_xattn_Wq).T,
        "WkvT": np.asarray(L0_xattn_Wkv).T,
        "WcT": np.asarray(L0_xattn_Wc).T,
        "routerT": np.asarray(L0_ffn_router_w).T,
        "w": np.concatenate([
            np.asarray(L0_ffn_w1).transpose(0, 2, 1).reshape(E, DC, P, 2, CW).transpose(0, 1, 3, 2, 4).reshape(E, WC1, P, CW),
            np.asarray(L0_ffn_w2).transpose(0, 2, 1).reshape(E, WC2, 2, P, D).transpose(0, 1, 3, 2, 4).reshape(E, WC2, P, CW),
        ], 1).reshape(NC, P, CW),
    }
    arrays, args = {}, {}
    for name, a in laid.items():
        arrays[f"in_{name}"] = np.ascontiguousarray(a)
        args[name] = nc.dram_tensor(f"in_{name}", a.shape, mybir.dt.from_np(a.dtype), kind="ExternalInput").ap()
    args["out"] = nc.dram_tensor("out_x", [B * S + P, D], F32, kind="ExternalOutput").ap()
    build(nc, **args)
    r = run_bass_kernel_spmd(nc, [arrays], core_ids=[0])
    return r.results[0]["out_x"][0:B * S].reshape(B, S, D)
```
